# Optimizing a Trainium2 kernel written in Bass

```python
import numpy as np
import jax
import jax.numpy as jnp

def _softmax(x, axis=-1):
    return jax.nn.softmax(x, axis=axis)

def _gelu(x):
    return jax.nn.gelu(x, approximate=True)

def _silu(x):
    return jax.nn.silu(x)

def _sigmoid(x):
    return jax.nn.sigmoid(x)

def _layernorm(x, axis=-1, eps=1e-05):
    m = jnp.mean(x, axis=axis, keepdims=True)
    v = jnp.var(x, axis=axis, keepdims=True)
    return (x - m) / jnp.sqrt(v + eps)

def _scatter_add(tgt, idx, src, axis=0):
    return tgt.at[idx].add(src)

def _segment_sum(src, seg, n):
    return jax.ops.segment_sum(src, seg, n)
kernel_name = 'mk_dlrm_tower_d1_rec_r8_085133'

def setup_inputs(seed: int=0):
    np.random.seed(seed)
    _w = jnp.asarray

    def _rec_inputs():
        import jax
        import jax.numpy as jnp
        _tk = jax.random.key(seed)
        ids = jnp.stack([jax.random.randint(jax.random.fold_in(_tk, 200 + f), (512,), 0, v, jnp.int32) for f, v in enumerate([1250, 1250, 12500, 125000, 125000, 12500, 125000, 12500, 1250, 12500, 1000, 1000, 1000, 12500, 1000, 12500, 1000, 12500, 1250, 1000, 1250, 1000, 1000, 12500, 1250, 1250])], axis=1)
        tbl_0 = 0.05 * jax.random.normal(jax.random.fold_in(_tk, 500 + 0), (1250, 64), jnp.float32)
        tbl_1 = 0.05 * jax.random.normal(jax.random.fold_in(_tk, 500 + 1), (1250, 64), jnp.float32)
        tbl_2 = 0.05 * jax.random.normal(jax.random.fold_in(_tk, 500 + 2), (12500, 64), jnp.float32)
        tbl_3 = 0.05 * jax.random.normal(jax.random.fold_in(_tk, 500 + 3), (125000, 64), jnp.float32)
        tbl_4 = 0.05 * jax.random.normal(jax.random.fold_in(_tk, 500 + 4), (125000, 64), jnp.float32)
        tbl_5 = 0.05 * jax.random.normal(jax.random.fold_in(_tk, 500 + 5), (12500, 64), jnp.float32)
        tbl_6 = 0.05 * jax.random.normal(jax.random.fold_in(_tk, 500 + 6), (125000, 64), jnp.float32)
        tbl_7 = 0.05 * jax.random.normal(jax.random.fold_in(_tk, 500 + 7), (12500, 64), jnp.float32)
        tbl_8 = 0.05 * jax.random.normal(jax.random.fold_in(_tk, 500 + 8), (1250, 64), jnp.float32)
        tbl_9 = 0.05 * jax.random.normal(jax.random.fold_in(_tk, 500 + 9), (12500, 64), jnp.float32)
        tbl_10 = 0.05 * jax.random.normal(jax.random.fold_in(_tk, 500 + 10), (1000, 64), jnp.float32)
        tbl_11 = 0.05 * jax.random.normal(jax.random.fold_in(_tk, 500 + 11), (1000, 64), jnp.float32)
        tbl_12 = 0.05 * jax.random.normal(jax.random.fold_in(_tk, 500 + 12), (1000, 64), jnp.float32)
        tbl_13 = 0.05 * jax.random.normal(jax.random.fold_in(_tk, 500 + 13), (12500, 64), jnp.float32)
        tbl_14 = 0.05 * jax.random.normal(jax.random.fold_in(_tk, 500 + 14), (1000, 64), jnp.float32)
        tbl_15 = 0.05 * jax.random.normal(jax.random.fold_in(_tk, 500 + 15), (12500, 64), jnp.float32)
        tbl_16 = 0.05 * jax.random.normal(jax.random.fold_in(_tk, 500 + 16), (1000, 64), jnp.float32)
        tbl_17 = 0.05 * jax.random.normal(jax.random.fold_in(_tk, 500 + 17), (12500, 64), jnp.float32)
        tbl_18 = 0.05 * jax.random.normal(jax.random.fold_in(_tk, 500 + 18), (1250, 64), jnp.float32)
        tbl_19 = 0.05 * jax.random.normal(jax.random.fold_in(_tk, 500 + 19), (1000, 64), jnp.float32)
        tbl_20 = 0.05 * jax.random.normal(jax.random.fold_in(_tk, 500 + 20), (1250, 64), jnp.float32)
        tbl_21 = 0.05 * jax.random.normal(jax.random.fold_in(_tk, 500 + 21), (1000, 64), jnp.float32)
        tbl_22 = 0.05 * jax.random.normal(jax.random.fold_in(_tk, 500 + 22), (1000, 64), jnp.float32)
        tbl_23 = 0.05 * jax.random.normal(jax.random.fold_in(_tk, 500 + 23), (12500, 64), jnp.float32)
        tbl_24 = 0.05 * jax.random.normal(jax.random.fold_in(_tk, 500 + 24), (1250, 64), jnp.float32)
        tbl_25 = 0.05 * jax.random.normal(jax.random.fold_in(_tk, 500 + 25), (1250, 64), jnp.float32)
        _rk = jax.random.fold_in(_tk, 7)
        r_dense_t = 7.22013e-05 + 1.00017 * jax.random.normal(jax.random.fold_in(_rk, 101), (512, 256), jnp.float32)
        W_top1 = 0.0360844 * jax.random.normal(jax.random.fold_in(_tk, 801), (768, 512), jnp.float32)
        W_top2 = 0.0441942 * jax.random.normal(jax.random.fold_in(_tk, 802), (512, 256), jnp.float32)
        W_top3 = 0.0625 * jax.random.normal(jax.random.fold_in(_tk, 803), (256, 1), jnp.float32)
        b_top1 = jnp.zeros((512,), jnp.float32)
        b_top2 = jnp.zeros((256,), jnp.float32)
        return (r_dense_t, ids, tbl_0, tbl_1, tbl_2, tbl_3, tbl_4, tbl_5, tbl_6, tbl_7, tbl_8, tbl_9, tbl_10, tbl_11, tbl_12, tbl_13, tbl_14, tbl_15, tbl_16, tbl_17, tbl_18, tbl_19, tbl_20, tbl_21, tbl_22, tbl_23, tbl_24, tbl_25, W_top1, b_top1, W_top2, b_top2, W_top3)
    r_dense_t, ids, tbl_0, tbl_1, tbl_2, tbl_3, tbl_4, tbl_5, tbl_6, tbl_7, tbl_8, tbl_9, tbl_10, tbl_11, tbl_12, tbl_13, tbl_14, tbl_15, tbl_16, tbl_17, tbl_18, tbl_19, tbl_20, tbl_21, tbl_22, tbl_23, tbl_24, tbl_25, W_top1, b_top1, W_top2, b_top2, W_top3 = _rec_inputs()

    def _L0_rec_setup():
        import jax, jax.numpy as jnp
        import numpy as np
        EPS = 1e-05
        NI = 33
        TRIL_I, TRIL_J = np.tril_indices(NI, k=-1)

        def layer_norm(x, g, b):
            m = jnp.mean(x, axis=-1, keepdims=True)
            v = jnp.mean(jnp.square(x - m), axis=-1, keepdims=True)
            return (x - m) * jax.lax.rsqrt(v + EPS) * g + b
        key = jax.random.key(seed)
        ks = jax.random.split(key, 8)
        B, D_DENSE, N_SP, D_SP = (4096, 256, 26, 64)
        E, PROJ, MAXD, NFLAT = (128, 32, 512, 528)
        dense_t = jax.random.normal(ks[0], (B, D_DENSE), dtype=jnp.float32)
        sparse_t = jax.random.normal(ks[1], (B, N_SP, D_SP), dtype=jnp.float32)
        Wd = jax.random.normal(ks[2], (E, D_DENSE), dtype=jnp.float32) / np.sqrt(D_DENSE)
        Ws = jax.random.normal(ks[3], (E, D_SP), dtype=jnp.float32) / np.sqrt(D_SP)
        Wsi = jax.random.normal(ks[4], (PROJ, N_SP), dtype=jnp.float32) / np.sqrt(N_SP)
        Wl = jax.random.normal(ks[5], (MAXD, NFLAT), dtype=jnp.float32) / np.sqrt(NFLAT)
        gd = jnp.ones((E,), jnp.float32)
        bd = jnp.zeros((E,), jnp.float32)
        gs = jnp.ones((E,), jnp.float32)
        bs = jnp.zeros((E,), jnp.float32)
        gsi = jnp.ones((PROJ,), jnp.float32)
        bsi = jnp.zeros((PROJ,), jnp.float32)
        gl = jnp.ones((MAXD,), jnp.float32)
        bl = jnp.zeros((MAXD,), jnp.float32)
        return {'dense_t': dense_t, 'sparse_t': sparse_t, 'Wd': Wd, 'gd': gd, 'bd': bd, 'Ws': Ws, 'gs': gs, 'bs': bs, 'Wsi': Wsi, 'gsi': gsi, 'bsi': bsi, 'Wl': Wl, 'gl': gl, 'bl': bl, 'dims_in_use': 384}
    _L0_rec_all = _L0_rec_setup()
    _L0_rec_in = {k: v for k, v in _L0_rec_all.items() if k in ('Wd', 'gd', 'bd', 'Ws', 'gs', 'bs', 'Wsi', 'gsi', 'bsi', 'Wl', 'gl', 'bl')}
    del _L0_rec_all
    return {'r_dense_t': r_dense_t, 'ids': ids, 'tbl_0': tbl_0, 'tbl_1': tbl_1, 'tbl_2': tbl_2, 'tbl_3': tbl_3, 'tbl_4': tbl_4, 'tbl_5': tbl_5, 'tbl_6': tbl_6, 'tbl_7': tbl_7, 'tbl_8': tbl_8, 'tbl_9': tbl_9, 'tbl_10': tbl_10, 'tbl_11': tbl_11, 'tbl_12': tbl_12, 'tbl_13': tbl_13, 'tbl_14': tbl_14, 'tbl_15': tbl_15, 'tbl_16': tbl_16, 'tbl_17': tbl_17, 'tbl_18': tbl_18, 'tbl_19': tbl_19, 'tbl_20': tbl_20, 'tbl_21': tbl_21, 'tbl_22': tbl_22, 'tbl_23': tbl_23, 'tbl_24': tbl_24, 'tbl_25': tbl_25, 'W_top1': W_top1, 'b_top1': b_top1, 'W_top2': W_top2, 'b_top2': b_top2, 'W_top3': W_top3, 'L0_rec_Wd': _L0_rec_in['Wd'], 'L0_rec_gd': _L0_rec_in['gd'], 'L0_rec_bd': _L0_rec_in['bd'], 'L0_rec_Ws': _L0_rec_in['Ws'], 'L0_rec_gs': _L0_rec_in['gs'], 'L0_rec_bs': _L0_rec_in['bs'], 'L0_rec_Wsi': _L0_rec_in['Wsi'], 'L0_rec_gsi': _L0_rec_in['gsi'], 'L0_rec_bsi': _L0_rec_in['bsi'], 'L0_rec_Wl': _L0_rec_in['Wl'], 'L0_rec_gl': _L0_rec_in['gl'], 'L0_rec_bl': _L0_rec_in['bl']}

def reference(r_dense_t, ids, tbl_0, tbl_1, tbl_2, tbl_3, tbl_4, tbl_5, tbl_6, tbl_7, tbl_8, tbl_9, tbl_10, tbl_11, tbl_12, tbl_13, tbl_14, tbl_15, tbl_16, tbl_17, tbl_18, tbl_19, tbl_20, tbl_21, tbl_22, tbl_23, tbl_24, tbl_25, W_top1, b_top1, W_top2, b_top2, W_top3, L0_rec_Wd, L0_rec_gd, L0_rec_bd, L0_rec_Ws, L0_rec_gs, L0_rec_bs, L0_rec_Wsi, L0_rec_gsi, L0_rec_bsi, L0_rec_Wl, L0_rec_gl, L0_rec_bl):
    import jax
    import jax.numpy as jnp

    def _L0_rec_ref(dense_t, sparse_t, Wd, gd, bd, Ws, gs, bs, Wsi, gsi, bsi, Wl, gl, bl, dims_in_use):
        import jax, jax.numpy as jnp
        import numpy as np
        EPS = 1e-05
        NI = 33
        TRIL_I, TRIL_J = np.tril_indices(NI, k=-1)

        def layer_norm(x, g, b):
            m = jnp.mean(x, axis=-1, keepdims=True)
            v = jnp.mean(jnp.square(x - m), axis=-1, keepdims=True)
            return (x - m) * jax.lax.rsqrt(v + EPS) * g + b
        x = layer_norm(dense_t @ Wd.T, gd, bd)
        y = layer_norm(jnp.einsum('bnd,ed->bne', sparse_t, Ws), gs, bs)
        y = jnp.einsum('bne,pn->bep', y, Wsi)
        y = layer_norm(y, gsi, bsi)
        y = jnp.swapaxes(y, 1, 2)
        T = jnp.concatenate([x[:, None, :], y], axis=1)
        Z = jnp.einsum('bnd,bmd->bnm', T, T)
        Zflat = Z[:, TRIL_I, TRIL_J]
        out = layer_norm(Zflat @ Wl.T, gl, bl)
        maxd = out.shape[-1]
        mask = (jnp.arange(maxd) < dims_in_use).astype(out.dtype)
        return out * mask
    e = jnp.stack([tbl_0[ids[:, 0]], tbl_1[ids[:, 1]], tbl_2[ids[:, 2]], tbl_3[ids[:, 3]], tbl_4[ids[:, 4]], tbl_5[ids[:, 5]], tbl_6[ids[:, 6]], tbl_7[ids[:, 7]], tbl_8[ids[:, 8]], tbl_9[ids[:, 9]], tbl_10[ids[:, 10]], tbl_11[ids[:, 11]], tbl_12[ids[:, 12]], tbl_13[ids[:, 13]], tbl_14[ids[:, 14]], tbl_15[ids[:, 15]], tbl_16[ids[:, 16]], tbl_17[ids[:, 17]], tbl_18[ids[:, 18]], tbl_19[ids[:, 19]], tbl_20[ids[:, 20]], tbl_21[ids[:, 21]], tbl_22[ids[:, 22]], tbl_23[ids[:, 23]], tbl_24[ids[:, 24]], tbl_25[ids[:, 25]]], axis=1)
    z = _L0_rec_ref(r_dense_t, e, L0_rec_Wd, L0_rec_gd, L0_rec_bd, L0_rec_Ws, L0_rec_gs, L0_rec_bs, L0_rec_Wsi, L0_rec_gsi, L0_rec_bsi, L0_rec_Wl, L0_rec_gl, L0_rec_bl, 384)
    z = z.reshape(z.shape[0], -1)
    h = jnp.concatenate([z, r_dense_t], axis=1)
    h = jnp.maximum(h @ W_top1 + b_top1, 0.0)
    h = jnp.maximum(h @ W_top2 + b_top2, 0.0)
    y = h @ W_top3
    return y

_drawn_inputs = setup_inputs


def setup_inputs(seed=0):
    import zlib

    import numpy as np

    out = dict(_drawn_inputs(seed))
    spreads = {'b_top1': (0.0, 0.1),
     'b_top2': (0.0, 0.1),
     'L0_rec_gd': (1.0, 0.6),
     'L0_rec_bd': (0.0, 0.8),
     'L0_rec_gs': (1.0, 0.6),
     'L0_rec_bs': (0.0, 0.1),
     'L0_rec_gsi': (1.0, 0.2),
     'L0_rec_bsi': (0.0, 0.1),
     'L0_rec_gl': (1.0, 0.2),
     'L0_rec_bl': (0.0, 0.1)}
    factors = {}
    for name, (base, spread) in spreads.items():
        noise = np.random.default_rng([zlib.crc32(name.encode()), seed]).standard_normal(out[name].shape)
        drawn = base * np.exp(spread * noise) if base else spread * noise
        out[name] = jnp.asarray(drawn.astype(out[name].dtype))
    for name, factor in factors.items():
        out[name] = (out[name] * factor).astype(out[name].dtype)
    return out
```

```python
from contextlib import ExitStack

import numpy as np
import concourse.bass as bass
from concourse import mybir

F32 = mybir.dt.float32
BF16 = mybir.dt.bfloat16
F16 = mybir.dt.float16
I32 = mybir.dt.int32
ALU = mybir.AluOpType
ACT = mybir.ActivationFunctionType
AX = mybir.AxisListType

P = 128
B = 512
NF = 26
D = 64
E = 128
PR = 32
DD = 256
MAXD = 512
USED = 384
H1 = 512
H2 = 256
EPS = 1e-5

TILE = 128
NT = B // TILE
HALF = TILE // 2
NCH = HALF * NF // P
UR = 16
UPT = HALF // UR
NU = NT * UPT
CHUNKS = [range(0 if m == 0 else (UR * m * NF - 1) // P + 1, (UR * (m + 1) * NF - 1) // P + 1)
          for m in range(UPT)]
ROWS_OF = [(P * c // NF, (P * c + P - 1) // NF) for c in range(NCH)]
SW = 6
YC = 2 + PR
GC = PR + 1
NG = PR // 4
GSL = 2 * UR // 4
KD = USED // P
KR = DD // P
KW = KD + KR

PACK_A = [("ident", P), ("block", P), ("wst", E), ("wssel", NCH * PR), ("selmask", NCH * SW), ("eps", 1)]
PACK_B = [("gsrep", E), ("bsrep", E), ("wsirep", PR * NF), ("mask9", 6), ("gd", 1), ("bd", 1),
          ("gi", 1), ("bi", 1), ("gj", NG), ("bj", NG), ("isi", PR), ("isj", NG * PR), ("isx", NG),
          ("b1", H1 // P), ("b2", H2 // P), ("gl", KD), ("bl", KD), ("w3", H2 // P)]


def columns(pack):
    at, out = 0, {}
    for name, n in pack:
        out[name] = (at, at + n)
        at += n
    return out, at


COL_A, NA = columns(PACK_A)
COL_B, NB = columns(PACK_B)


def build(nc, table, lookups, starts, pack_a, pack_b, wdt, denset, wlt, w1, w2, out):
    with ExitStack() as ctx:
        def sb(name, shape, dt=F32):
            return ctx.enter_context(nc.sbuf_tensor(name, shape, dt))

        def ps(name, shape):
            return ctx.enter_context(nc.psum_tensor(name, shape, F32))

        def sem(name):
            return ctx.enter_context(nc.semaphore(name))

        a_sb = sb("a_sb", [P, NA])
        b_sb = sb("b_sb", [P, NB])

        def pa(name, rows=slice(0, P)):
            lo, hi = COL_A[name]
            return a_sb[rows, lo:hi]

        def pb(name, rows=slice(0, P)):
            lo, hi = COL_B[name]
            return b_sb[rows, lo:hi]

        rel = sb("rel", [P, NT, NCH, 2], I32)
        first = sb("first", [P, NT, NCH, 2], I32)
        idx = sb("idx", [P, NT * NCH * 2], I32)
        emb = sb("emb", [P, NT * NCH * 2, D])
        prod = sb("prod", [P, 8 * D])
        var = sb("var", [P, NT * NCH * 2])
        std = sb("std", [P, NT * NCH * 2])
        inv = sb("inv", [P, NT * NCH * 2])
        embt = [sb(f"embt{i}", [P, 4 * P]) for i in range(2)]
        wt = [sb(f"wt{i}", [P, 2, UR * PR], F16) for i in range(2)]
        sq = sb("sq", [P, 2 * UR * PR])
        vary = [sb(f"vary{i}", [P, 2 * UR]) for i in range(2)]
        stdy = [sb(f"stdy{i}", [P, 2 * UR]) for i in range(2)]
        invy = [sb(f"invy{i}", [P, 2 * UR]) for i in range(2)]
        tt = sb("tt", [P, B, YC])
        zs = [sb(f"zs{i}", [P, NG, TILE]) for i in range(2)]
        zx = sb("zx", [P, B])
        wl = sb("wl", [P, NG, MAXD])
        wx = sb("wx", [P, MAXD])
        mx = sb("mx", [P, NG, 96])
        mxt = sb("mxt", [P, NG, PR])
        w1s = sb("w1s", [P, KW, H1])
        w2s = sb("w2s", [P, H1 // P, H2])
        wds = sb("wds", [P, KR, E])
        dts = sb("dts", [P, KR, B])
        wm = sb("wm", [P, NCH])
        wsel = sb("wsel", [P, NCH, PR])
        sel = sb("sel", [P, NCH, SW, PR])
        mean1 = sb("mean1", [P, 1])
        wsc = sb("wsc", [P, E])
        wsce = sb("wsce", [P, P])
        g2 = sb("g2", [P, P])
        wvf = sb("wvf", [P, E])
        wvh = sb("wvh", [P, E], F16)
        wvl = sb("wvl", [P, E], F16)
        rest = sb("rest", [P, E + PR])
        part = [sb(f"part{i}", [P, E + PR], BF16) for i in range(3)]
        pick = [sb(f"pick{i}", [P, E + PR], BF16) for i in range(2)]
        bs9 = sb("bs9", [P, E], BF16)
        ws9 = sb("ws9", [P, PR], BF16)
        ws9r = sb("ws9r", [P, UR, PR], BF16)
        wsum = sb("wsum", [P, PR])
        wmean = sb("wmean", [P, 1])
        xst = sb("xst", [P, NT, 6])
        xmv = sb("xmv", [P, NT, 2])
        xstd = sb("xstd", [P, NT])
        xinv = sb("xinv", [P, NT])
        xn = sb("xn", [P, NT, E])
        gibj = sb("gibj", [P, NG])
        gjbi = sb("gjbi", [P, NG])
        gij = sb("gij", [P, NG])
        b1e = sb("b1e", [P, H1 // P])
        ost = sb("ost", [P, 6])
        omv = sb("omv", [P, 2])
        ostd = sb("ostd", [P, 1])
        oinv = sb("oinv", [P, 1])
        onmr = sb("onmr", [P, 1])
        zn = sb("zn", [P, USED])
        znt = sb("znt", [P, KD, TILE])
        h1 = sb("h1", [P, H1 // P, TILE])
        h2 = sb("h2", [P, H2 // P, TILE])
        yrow = sb("yrow", [1, B])

        pq = ps("pq", [P, 4 * P])
        pw = [ps(f"pw{i}", [P, 512]) for i in range(2)]
        pv = ps("pv", [P, 2, 512])
        pg = ps("pg", [P, 2, 512])
        po = ps("po", [P, 512])

        ld_rel, ld_first, ld_a, ld_b, ld_x, ld_wl, ld_w1, ld_w2, ld_dt = (
            sem(n) for n in ("ld_rel", "ld_first", "ld_a", "ld_b", "ld_x", "ld_wl", "ld_w1", "ld_w2", "ld_dt"))
        idx_ready = sem("idx_ready")
        gathered = [sem(f"gathered{u}") for u in range(NU)]
        setup_v = sem("setup_v")
        setup_pe = sem("setup_pe")
        setup_a = sem("setup_a")
        tr_done, embt_ready, q_done, prod_ready, var_ready, std_ready, inv_ready, scaled = (
            sem(n) for n in ("tr_done", "embt_ready", "q_done", "prod_ready", "var_ready", "std_ready",
                             "inv_ready", "scaled"))
        contracted, hi_ready, wt_ready, v_done, sq_ready, vary_ready, stdy_ready, invy_ready, t_ready = (
            sem(n) for n in ("contracted", "hi_ready", "wt_ready", "v_done", "sq_ready", "vary_ready", "stdy_ready",
                             "invy_ready", "t_ready"))
        gram_done, z_ready = sem("gram_done"), sem("z_ready")
        o_done, ost_ready, omv_ready, ostd_ready, oinv_ready, onmr_ready, zn_ready, znt_done, znt_ready = (
            sem(n) for n in ("o_done", "ost_ready", "omv_ready", "ostd_ready", "oinv_ready", "onmr_ready",
                             "zn_ready", "znt_done", "znt_ready"))
        h1_done, h1_ready, h2_done, h2_ready, y_done, y_ready = (
            sem(n) for n in ("h1_done", "h1_ready", "h2_done", "h2_ready", "y_done", "y_ready"))
        stored = sem("stored")

        def kof(u):
            t, m = divmod(u, UPT)
            return (t * NCH + CHUNKS[m][0]) * 2, 2 * len(CHUNKS[m])

        block = ctx.enter_context(nc.Block())

        @block.sync
        def _(sp):
            sp.dma_start(rel[:, :, :, :], lookups).then_inc(ld_rel, 16)
            sp.dma_start(first[:, :, :, :], starts).then_inc(ld_first, 16)
            sp.dma_start(a_sb[:, :], pack_a).then_inc(ld_a, 16)
            sp.dma_start(b_sb[:, :], pack_b).then_inc(ld_b, 16)
            sp.dma_start(wds[:, :, :], wdt).then_inc(ld_x, 16)
            sp.dma_start(dts[:, :, :], denset).then_inc(ld_dt, 16)
            sp.dma_start(wl[:, :, :], wlt).then_inc(ld_wl, 16)
            sp.dma_start(w1s[:, :, :], w1).then_inc(ld_w1, 16)
            sp.dma_start(w2s[:, :, :], w2).then_inc(ld_w2, 16)
            sp.wait_ge(y_ready, NT)
            sp.dma_start(out, yrow[:, :]).then_inc(stored, 16)
            sp.wait_ge(stored, 16)

        @block.gpsimd
        def _(pool):
            pool.wait_ge(ld_rel, 16)
            pool.wait_ge(ld_first, 16)
            pool.tensor_tensor(idx[:, :], rel[:, :, :, :].rearrange("p t c s -> p (t c s)"),
                               first[:, :, :, :].rearrange("p t c s -> p (t c s)"), ALU.add).then_inc(idx_ready, 1)
            pool.wait_ge(idx_ready, 1)
            for u in range(NU):
                k0, nk = kof(u)
                for k in range(k0, k0 + nk):
                    pool.indirect_dma_start(emb[:, k, :], None, table,
                                            bass.IndirectOffsetOnAxis(ap=idx[:, k:k + 1], axis=0)
                                            ).then_inc(gathered[u], 16)

        def numbered(*names):
            return {n: i + 1 for i, n in enumerate(names)}

        V = numbered(
            "wsum1", "wmean1", "wsc", "selsum", "selmean", "selc", "sel", "g2", "xst", "xmv", "xinv", "xn",
            "wvf", "wvh", "wvl", "wsum", "wsumsum", "wmean", "rest0", "rest1", "part0", "left0", "part1",
            "left1", "part2", "bs9_0", "ws9_0", "bs9_1", "ws9_1", "bs9_2", "ws9_2", "ws9r", "ones", "zx0",
            "zx1", "xt", "mxz", "wxz", "gibj", "gjbi", "gij", "mxi", "mxj", "mxs", "mxx", "mx", "b1e", "wls",
            "w1s")
        PES = numbered("wsct", "g", "x", "xt", "xs", "wx", "b1")
        AS = numbered("wsce", "xstd", "xs", "wx")

        @block.tensor
        def _(pe):
            def transposes(u):
                k0, nk = kof(u)
                pe.wait_ge(gathered[u], 16 * nk)
                if u:
                    pe.wait_ge(prod_ready, u)
                for c in range(nk // 2):
                    mm = pe.transpose(pq[:, c * P:(c + 1) * P],
                                      emb[:, k0 + 2 * c:k0 + 2 * c + 2, :].rearrange("p s d -> p (s d)"), pa("ident"))
                mm.then_inc(tr_done, 1)

            def quadratic(u):
                pe.wait_ge(embt_ready, u + 1)
                _, nk = kof(u)
                for c in range(nk // 2):
                    mm = pe.matmul(pq[:, c * P:(c + 1) * P], embt[u % 2][:, c * P:(c + 1) * P], g2[:, :],
                                   start=True, stop=True)
                mm.then_inc(q_done, 1)

            def contract(u):
                t, m = divmod(u, UPT)
                pe.wait_ge(scaled, u + 1)
                if u:
                    pe.wait_ge(wt_ready, u)
                for c in CHUNKS[m]:
                    b0, b1 = ROWS_OF[c]
                    k = (t * NCH + c) * 2
                    lhs = emb[:, k:k + 2, :].rearrange("p s d -> p (s d)")
                    for mm_ in (m, m + 1):
                        lo, hi = max(b0, UR * mm_), min(b1 + 1, UR * (mm_ + 1))
                        if lo >= hi:
                            continue
                        mm = pe.matmul(pw[(t * UPT + mm_) % 2][:, (lo - UR * mm_) * PR:(hi - UR * mm_) * PR],
                                       lhs, sel[:, c, lo - b0:hi - b0, :].rearrange("p j q -> p (j q)"),
                                       start=(mm_ > m or (m == 0 and c == 0)), stop=True, skip_group_check=True)
                mm.then_inc(contracted, 1)

            def expand(u):
                pe.wait_ge(wt_ready, u + 1)
                if u:
                    pe.wait_ge(t_ready, u)
                for s in range(2):
                    pe.matmul(pv[:, s, :], wvh[:, :], wt[u % 2][:, s, :], start=True, stop=False)
                    pe.matmul(pv[:, s, :], wvl[:, :], wt[u % 2][:, s, :], start=False, stop=False)
                    mm = pe.matmul(pv[:, s, :], bs9[:, :], ws9r[:, :, :].rearrange("p b q -> p (b q)"),
                                   start=False, stop=True)
                mm.then_inc(v_done, 1)

            def gram(u):
                t, m = divmod(u, UPT)
                pe.wait_ge(t_ready, u + 1)
                if u >= 2 and u % 2 == 0:
                    pe.wait_ge(z_ready, u // 2)
                for s in range(2):
                    for j in range(UR):
                        b = t * TILE + s * HALF + UR * m + j
                        q, slot = j % 4, (m % 2) * 4 + j // 4
                        mm = pe.matmul(pg[32 * q:32 * q + 32, s, slot * GC:(slot + 1) * GC],
                                       tt[:, b, 2:YC], tt[:, b, 0:GC], start=True, stop=True)
                mm.then_inc(gram_done, 1)

            def flat_linear(t):
                pe.wait_ge(z_ready, 2 * t + 2)
                if t:
                    pe.wait_ge(y_ready, t)
                for g in range(NG):
                    pe.matmul(po[:, :], zs[t % 2][:, g, :], wl[:, g, :], start=(g == 0), stop=False)
                pe.matmul(po[:, :], zx[:, t * TILE:(t + 1) * TILE], wx[:, :], start=False, stop=True
                          ).then_inc(o_done, 1)

            def z_transposes(t):
                pe.wait_ge(zn_ready, t + 1)
                for c in range(KD):
                    mm = pe.transpose(po[:, c * P:(c + 1) * P], zn[:, c * P:(c + 1) * P], pa("ident"))
                mm.then_inc(znt_done, 1)

            def top1(t):
                pe.wait_ge(znt_ready, t + 1)
                for o in range(H1 // P):
                    for c in range(KW):
                        rhs = znt[:, c, :] if c < KD else dts[:, c - KD, t * TILE:(t + 1) * TILE]
                        mm = pe.matmul(po[:, o * P:(o + 1) * P], w1s[:, c, o * P:(o + 1) * P], rhs,
                                       start=(c == 0), stop=(c == KW - 1))
                mm.then_inc(h1_done, 1)

            def top2(t):
                pe.wait_ge(h1_ready, t + 1)
                for o in range(H2 // P):
                    for c in range(H1 // P):
                        mm = pe.matmul(po[:, o * P:(o + 1) * P], w2s[:, c, o * P:(o + 1) * P], h1[:, c, :],
                                       start=(c == 0), stop=(c == H1 // P - 1))
                mm.then_inc(h2_done, 1)

            def top3(t):
                pe.wait_ge(h2_ready, t + 1)
                for c in range(H2 // P):
                    mm = pe.matmul(po[0:1, 0:P], pb("w3")[:, c:c + 1], h2[:, c, :],
                                   start=(c == 0), stop=(c == H2 // P - 1))
                mm.then_inc(y_done, 1)

            pe.wait_ge(ld_a, 16)
            pe.wait_ge(setup_v, V["wsc"])
            pe.transpose(po[:, 0:P], wsc[:, :], pa("ident")).then_inc(setup_pe, 1)
            pe.wait_ge(setup_a, AS["wsce"])
            pe.matmul(po[:, 0:P], wsce[:, :], wsce[:, :], start=True, stop=True).then_inc(setup_pe, 1)
            pe.wait_ge(setup_v, V["g2"])
            pe.wait_ge(ld_x, 16)
            pe.wait_ge(ld_dt, 16)
            for t in range(NT):
                for c in range(KR):
                    mm = pe.matmul(po[:, t * E:(t + 1) * E], dts[:, c, t * TILE:(t + 1) * TILE], wds[:, c, :],
                                   start=(c == 0), stop=(c == KR - 1))
            mm.then_inc(setup_pe, 1)

            def x_transposes():
                pe.wait_ge(setup_v, V["xn"])
                for t in range(NT):
                    mm = pe.transpose(po[:, t * TILE:(t + 1) * TILE], xn[:, t, :], pa("ident"))
                mm.then_inc(setup_pe, 1)

            def x_sums():
                pe.wait_ge(setup_v, V["xt"])
                pe.matmul(po[32:33, 0:B], tt[:, 0, 0:1], tt[:, :, 1], start=True, stop=True).then_inc(setup_pe, 1)

            def late_setup():
                pe.wait_ge(setup_a, AS["xs"])
                pe.wait_ge(setup_v, V["mx"])
                pe.wait_ge(ld_wl, 16)
                for g in range(NG):
                    mm = pe.matmul(po[0:96, :], mx[:, g, :], wl[:, g, :], start=(g == 0), stop=(g == NG - 1))
                mm.then_inc(setup_pe, 1)
                pe.wait_ge(setup_a, AS["wx"])
                pe.wait_ge(ld_w1, 16)
                for o in range(H1 // P):
                    for c in range(KD):
                        mm = pe.matmul(po[:, o:o + 1], w1s[:, c, o * P:(o + 1) * P], pb("bl")[:, c:c + 1],
                                       start=(c == 0), stop=(c == KD - 1))
                mm.then_inc(setup_pe, 1)

            for i in range(NU + 3):
                t, m = divmod(i - 7, UPT)
                late = t >= 0
                if i < NU:
                    transposes(i)
                if 0 <= i - 1 < NU:
                    contract(i - 1)
                if i < NU:
                    quadratic(i)
                if i == 2:
                    x_sums()
                if 0 <= i - 2 < NU:
                    expand(i - 2)
                if i == 1:
                    x_transposes()
                if i == 3:
                    late_setup()
                if i == 5:
                    pe.wait_ge(setup_v, V["w1s"])
                    pe.wait_ge(ld_w2, 16)
                if late and m == 0:
                    flat_linear(t)
                if late and m == 1:
                    z_transposes(t)
                if late and m == 2:
                    top1(t)
                if late and m == 3:
                    top2(t)
                if 0 <= i - 3 < NU:
                    gram(i - 3)
                if late and m == 3:
                    top3(t)
            flat_linear(NT - 1)
            z_transposes(NT - 1)
            top1(NT - 1)
            top2(NT - 1)
            top3(NT - 1)

        def z_parts(h, q):
            t = h // 2
            b0 = 32 * (h % 2) + q
            src = pg[32 * q:32 * q + 32, :, 0:GSL * GC].rearrange("p s (l c) -> p s l c", c=GC)
            dst = zs[t % 2][:, :, :].rearrange("p g (s r) -> p s r g", s=2)
            return [(src[:, :, :, 1 + j:GC:4], dst[32 * j:32 * j + 32, :, b0:b0 + 29:4, :]) for j in range(4)]

        def zx_part(h, q):
            t = h // 2
            b0 = 32 * (h % 2) + q
            src = pg[32 * q:32 * q + 32, :, 0:GSL * GC].rearrange("p s (l c) -> p s l c", c=GC)[:, :, :, 0]
            dst = zx[0:32, t * TILE:(t + 1) * TILE].rearrange("p (s r) -> p s r", s=2)[:, :, b0:b0 + 29:4]
            return src, dst

        @block.scalar
        def _(act):
            def embt_copy(u):
                act.wait_ge(tr_done, u + 1)
                if u >= 2:
                    act.wait_ge(q_done, u - 1)
                _, nk = kof(u)
                n = nk // 2 * P
                act.activation(embt[u % 2][:, 0:n], pq[:, 0:n], ACT.Copy).then_inc(embt_ready, 1)

            def std_rows(u):
                k0, nk = kof(u)
                act.wait_ge(var_ready, u + 1)
                act.activation(std[:, k0:k0 + nk], var[:, k0:k0 + nk], ACT.Sqrt, bias=pa("eps")).then_inc(std_ready, 1)

            def wt_hi(u):
                act.wait_ge(contracted, u + 1)
                if u >= 2:
                    act.wait_ge(v_done, u - 1)
                for s in range(2):
                    here = slice(D * s, D * s + D)
                    act.activation(wt[u % 2][here, s, :], pw[u % 2][here, :], ACT.Copy).then_inc(hi_ready, 1)

            def squares(u):
                act.wait_ge(v_done, u + 1)
                if u:
                    act.wait_ge(vary_ready, u)
                act.activation(sq[:, :], pv[:, :, :].rearrange("p s c -> p (s c)"), ACT.Square,
                               scale=float(PR) ** -0.5).then_inc(sq_ready, 1)

            def std_y(u):
                act.wait_ge(vary_ready, u + 1)
                if u >= 2:
                    act.wait_ge(invy_ready, u - 1)
                act.activation(stdy[u % 2][:, :], vary[u % 2][:, :], ACT.Sqrt, bias=pa("eps")).then_inc(stdy_ready, 1)

            def z_copies(h):
                act.wait_ge(gram_done, 2 * h + 2)
                if h % 2 == 0 and h >= 4:
                    act.wait_ge(o_done, h // 2 - 1)
                for q in range(4):
                    for src, dst in z_parts(h, q):
                        act.activation(dst, src, ACT.Copy)
                    src, dst = zx_part(h, q)
                    last = act.activation(dst, src, ACT.Copy)
                last.then_inc(z_ready, 1)

            def normalise(t):
                act.wait_ge(omv_ready, t + 1)
                act.activation(ostd[:, :], omv[:, 1:2], ACT.Sqrt, bias=pa("eps")).then_inc(ostd_ready, 1)
                act.wait_ge(onmr_ready, t + 1)
                act.activation(zn[:, :], po[:, 0:USED], ACT.Identity, bias=onmr[:, :], scale=oinv[:, :]
                               ).then_inc(zn_ready, 1)

            def relu1(t):
                act.wait_ge(h1_done, t + 1)
                for o in range(H1 // P):
                    last = act.activation(h1[:, o, :], po[:, o * P:(o + 1) * P], ACT.Relu, bias=b1e[:, o:o + 1])
                last.then_inc(h1_ready, 1)

            def relu2(t):
                act.wait_ge(h2_done, t + 1)
                for o in range(H2 // P):
                    last = act.activation(h2[:, o, :], po[:, o * P:(o + 1) * P], ACT.Relu,
                                          bias=pb("b2")[:, o:o + 1])
                last.then_inc(h2_ready, 1)

            act.wait_ge(ld_a, 16)
            act.wait_ge(ld_b, 16)
            act.wait_ge(setup_pe, PES["wsct"])
            act.activation(wsce[:, :], po[:, 0:P], ACT.Copy).then_inc(setup_a, 1)
            for i in range(NU + 3):
                t, m = divmod(i - 7, UPT)
                late = t >= 0
                if i < NU:
                    embt_copy(i)
                if 0 <= i - 1 < NU:
                    wt_hi(i - 1)
                if i < NU:
                    std_rows(i)
                if i == 0:
                    act.wait_ge(setup_v, V["xmv"])
                    act.activation(xstd[:, :], xmv[:, :, 1], ACT.Sqrt, bias=pa("eps")).then_inc(setup_a, 1)
                if i == 2:
                    act.wait_ge(setup_pe, PES["xs"])
                    act.wait_ge(setup_v, V["zx1"])
                    act.activation(zx[32:33, :], po[32:33, 0:B], ACT.Copy).then_inc(setup_a, 1)
                if 0 <= i - 2 < NU:
                    squares(i - 2)
                    std_y(i - 2)
                if i == 3:
                    act.wait_ge(setup_pe, PES["wx"])
                    act.activation(wx[0:96, :], po[0:96, :], ACT.Copy).then_inc(setup_a, 1)
                if late and m == 3:
                    relu2(t)
                if i >= 4 and i % 2 == 0:
                    z_copies((i - 4) // 2)
                if late and m == 0:
                    normalise(t)
                if late and m == 2:
                    relu1(t)
            normalise(NT - 1)
            relu1(NT - 1)
            relu2(NT - 1)

        @block.vector
        def _(dve):
            def products(u):
                k0, nk = kof(u)
                dve.wait_ge(q_done, u + 1)
                if u:
                    dve.wait_ge(var_ready, u)
                dve.tensor_tensor(prod[:, 0:nk * D], pq[:, 0:nk * D],
                                  emb[:, k0:k0 + nk, :].rearrange("p k d -> p (k d)"), ALU.mult
                                  ).then_inc(prod_ready, 1)
                dve.wait_ge(prod_ready, u + 1)
                dve.tensor_reduce(var[:, k0:k0 + nk], prod[:, 0:nk * D].rearrange("p (k d) -> p k d", d=D),
                                  AX.X, ALU.add).then_inc(var_ready, 1)

            def scale_rows(u):
                k0, nk = kof(u)
                dve.wait_ge(std_ready, u + 1)
                dve.reciprocal(inv[:, k0:k0 + nk], std[:, k0:k0 + nk]).then_inc(inv_ready, 1)
                dve.wait_ge(inv_ready, u + 1)
                dve.tensor_tensor(emb[:, k0:k0 + nk, :], emb[:, k0:k0 + nk, :],
                                  inv[:, k0:k0 + nk].unsqueeze(2).broadcast_to([P, nk, D]), ALU.mult
                                  ).then_inc(scaled, 1)

            def wt_lo(u):
                for s in range(2):
                    dve.wait_ge(hi_ready, 2 * u + s + 1)
                    here, other = slice(D * s, D * s + D), slice(D * (1 - s), D * (1 - s) + D)
                    last = dve.tensor_tensor(wt[u % 2][other, s, :], pw[u % 2][here, :], wt[u % 2][here, s, :],
                                             ALU.subtract)
                last.then_inc(wt_ready, 1)

            def var_y(u):
                dve.wait_ge(sq_ready, u + 1)
                if u >= 2:
                    dve.wait_ge(stdy_ready, u - 1)
                dve.tensor_reduce(vary[u % 2][:, :], sq[:, :].rearrange("p (b q) -> p b q", q=PR),
                                  AX.X, ALU.add).then_inc(vary_ready, 1)

            def scale_y(u):
                t, m = divmod(u, UPT)
                dve.wait_ge(stdy_ready, u + 1)
                dve.reciprocal(invy[u % 2][:, :], stdy[u % 2][:, :]).then_inc(invy_ready, 1)
                dve.wait_ge(invy_ready, u + 1)
                for s in range(2):
                    b = t * TILE + s * HALF + UR * m
                    last = dve.tensor_tensor(
                        tt[:, b:b + UR, 2:YC], pv[:, s, :].rearrange("p (b q) -> p b q", q=PR),
                        invy[u % 2][:, s * UR:(s + 1) * UR].unsqueeze(2).broadcast_to([P, UR, PR]), ALU.mult)
                last.then_inc(t_ready, 1)

            def stats(t):
                dve.wait_ge(o_done, t + 1)
                dve.bn_stats(ost[:, :], po[:, :]).then_inc(ost_ready, 1)
                dve.wait_ge(ost_ready, t + 1)
                dve.bn_aggr(omv[:, :], ost[:, :]).then_inc(omv_ready, 1)
                dve.wait_ge(ostd_ready, t + 1)
                dve.reciprocal(oinv[:, :], ostd[:, :]).then_inc(oinv_ready, 1)
                dve.wait_ge(oinv_ready, t + 1)
                dve.scalar_tensor_tensor(out=onmr[:, :], in0=omv[:, 0:1], scalar=-1.0, in1=oinv[:, :],
                                         op0=ALU.mult, op1=ALU.mult).then_inc(onmr_ready, 1)

            def znt_copy(t):
                dve.wait_ge(znt_done, t + 1)
                if t:
                    dve.wait_ge(h1_done, t)
                dve.tensor_copy(znt[:, :, :].rearrange("p c b -> p (c b)"), po[:, 0:USED]).then_inc(znt_ready, 1)

            def y_copy(t):
                dve.wait_ge(y_done, t + 1)
                dve.tensor_copy(yrow[:, t * TILE:(t + 1) * TILE], po[0:1, 0:P]).then_inc(y_ready, 1)

            def done(name, ins):
                ins.then_inc(setup_v, 1)
                dve.wait_ge(setup_v, V[name])

            def setup_lookup():
                dve.wait_ge(ld_a, 16)
                done("wsum1", dve.tensor_reduce(mean1[:, :], pa("wst"), AX.X, ALU.add))
                done("wmean1", dve.tensor_scalar(mean1[:, :], mean1[:, :], 1.0 / E, None, ALU.mult))
                done("wsc", dve.tensor_scalar(wsc[:, :], pa("wst"), mean1[:, :], None, ALU.subtract))
                wssel = pa("wssel").rearrange("p (c q) -> p c q", q=PR)
                done("selsum", dve.tensor_reduce(wm[:, :], wssel, AX.X, ALU.add))
                done("selmean", dve.tensor_scalar(wm[:, :], wm[:, :], 1.0 / PR, None, ALU.mult))
                done("selc", dve.tensor_tensor(wsel[:, :, :], wssel,
                                               wm[:, :].unsqueeze(2).broadcast_to([P, NCH, PR]), ALU.subtract))
                done("sel", dve.tensor_tensor(
                    sel[:, :, :, :], wsel[:, :, :].unsqueeze(2).broadcast_to([P, NCH, SW, PR]),
                    pa("selmask").rearrange("p (c j) -> p c j", j=SW).unsqueeze(3).broadcast_to([P, NCH, SW, PR]),
                    ALU.mult))
                dve.wait_ge(setup_pe, PES["g"])
                done("g2", dve.tensor_tensor(g2[:, :], po[:, 0:P], pa("block"), ALU.mult))

            def setup_x():
                dve.wait_ge(setup_pe, PES["x"])
                for t in range(NT):
                    last = dve.bn_stats(xst[:, t, :], po[:, t * E:(t + 1) * E])
                done("xst", last)
                for t in range(NT):
                    last = dve.bn_aggr(xmv[:, t, :], xst[:, t, :])
                done("xmv", last)
                dve.wait_ge(setup_a, AS["xstd"])
                done("xinv", dve.reciprocal(xinv[:, :], xstd[:, :]))
                for t in range(NT):
                    last = dve.tensor_scalar(xn[:, t, :], po[:, t * E:(t + 1) * E], xmv[:, t, 0:1],
                                             xinv[:, t:t + 1], ALU.subtract, ALU.mult)
                done("xn", last)

            def setup_expand():
                dve.wait_ge(ld_b, 16)
                done("wvf", dve.tensor_tensor(wvf[:, :], wsc[:, :], pb("gsrep"), ALU.mult))
                done("wvh", dve.tensor_copy(wvh[:, :], wvf[:, :]))
                done("wvl", dve.tensor_tensor(wvl[:, :], wvf[:, :], wvh[:, :], ALU.subtract))
                done("wsum", dve.tensor_reduce(wsum[:, :], pb("wsirep").rearrange("p (q n) -> p q n", n=NF),
                                               AX.X, ALU.add))
                done("wsumsum", dve.tensor_reduce(wmean[:, :], wsum[:, :], AX.X, ALU.add))
                done("wmean", dve.tensor_scalar(wmean[:, :], wmean[:, :], 1.0 / PR, None, ALU.mult))
                done("rest0", dve.tensor_scalar(rest[:, E:E + PR], wsum[:, :], wmean[:, :], None, ALU.subtract))
                done("rest1", dve.tensor_copy(rest[:, 0:E], pb("bsrep")))
                for i in range(3):
                    done(f"part{i}", dve.tensor_copy(part[i][:, :], rest[:, :]))
                    if i < 2:
                        done(f"left{i}", dve.tensor_tensor(rest[:, :], rest[:, :], part[i][:, :], ALU.subtract))
                m9 = pb("mask9")
                done("bs9_0", dve.tensor_scalar(bs9[:, :], part[0][:, 0:E], m9[:, 0:1], None, ALU.mult))
                done("ws9_0", dve.tensor_scalar(ws9[:, :], part[0][:, E:E + PR], m9[:, 3:4], None, ALU.mult))
                for i in (1, 2):
                    done(f"bs9_{i}", dve.scalar_tensor_tensor(
                        out=bs9[:, :], in0=part[i][:, 0:E], scalar=m9[:, i:i + 1], in1=bs9[:, :],
                        op0=ALU.mult, op1=ALU.add))
                    done(f"ws9_{i}", dve.scalar_tensor_tensor(
                        out=ws9[:, :], in0=part[i][:, E:E + PR], scalar=m9[:, 3 + i:4 + i], in1=ws9[:, :],
                        op0=ALU.mult, op1=ALU.add))
                done("ws9r", dve.tensor_copy(ws9r[:, :, :], ws9[:, :].unsqueeze(1).broadcast_to([P, UR, PR])))

            def setup_z():
                done("ones", dve.memset(tt[:, :, 0], 1.0))
                done("zx0", dve.memset(zx[:, :], 0.0))
                done("zx1", dve.memset(zx[64:65, :], 1.0))
                dve.wait_ge(setup_pe, PES["xt"])
                done("xt", dve.tensor_scalar(tt[:, :, 1], po[:, :], pb("gd"), pb("bd"), ALU.mult, ALU.add))
                done("mxz", dve.memset(mx[:, :, :], 0.0))
                done("wxz", dve.memset(wx[96:P, :], 0.0))
                done("gibj", dve.tensor_scalar(gibj[:, :], pb("bj"), pb("gi"), None, ALU.mult))
                done("gjbi", dve.tensor_scalar(gjbi[:, :], pb("gj"), pb("bi"), None, ALU.mult))
                done("gij", dve.tensor_scalar(gij[:, :], pb("gj"), pb("gi"), None, ALU.mult))
                done("mxi", dve.tensor_tensor(mxt[:, :, :], pb("isi").unsqueeze(1).broadcast_to([P, NG, PR]),
                                              gibj[:, :].unsqueeze(2).broadcast_to([P, NG, PR]), ALU.mult))
                done("mxj", dve.tensor_tensor(mx[:, :, 0:PR], pb("isj").rearrange("p (g q) -> p g q", q=PR),
                                              gjbi[:, :].unsqueeze(2).broadcast_to([P, NG, PR]), ALU.mult))
                done("mxs", dve.tensor_tensor(mx[:, :, 0:PR], mx[:, :, 0:PR], mxt[:, :, :], ALU.add))
                done("mxx", dve.tensor_scalar(mx[:, :, 32], pb("isx"), pb("bi"), None, ALU.mult))
                done("mx", dve.tensor_scalar(mx[:, :, 64], pb("bj"), pb("bi"), float(E), ALU.mult, ALU.mult))

            def late_setup():
                dve.wait_ge(setup_pe, PES["b1"])
                done("b1e", dve.tensor_tensor(b1e[:, :], po[:, 0:H1 // P], pb("b1"), ALU.add))
                for g in range(NG):
                    last = dve.tensor_scalar(wl[:, g, :], wl[:, g, :], gij[:, g:g + 1], None, ALU.mult)
                done("wls", last)
                for c in range(KD):
                    last = dve.tensor_scalar(w1s[:, c, :], w1s[:, c, :], pb("gl")[:, c:c + 1], None, ALU.mult)
                done("w1s", last)

            setup_lookup()
            for i in range(NU + 3):
                t, m = divmod(i - 7, UPT)
                late = t >= 0
                if i < NU:
                    products(i)
                if 0 <= i - 1 < NU:
                    wt_lo(i - 1)
                if i < NU:
                    scale_rows(i)
                if i == 0:
                    setup_x()
                if 0 <= i - 2 < NU:
                    var_y(i - 2)
                    scale_y(i - 2)
                if i == 0:
                    setup_expand()
                if i == 1:
                    setup_z()
                if i == 3:
                    late_setup()
                if late and m == 0:
                    stats(t)
                if late and m == 1:
                    znt_copy(t)
                if late and m == 3:
                    y_copy(t)
            stats(NT - 1)
            znt_copy(NT - 1)
            y_copy(NT - 1)


TABLES = [f"tbl_{f}" for f in range(NF)]


def kernel(**inputs):
    import numpy as _np
    import concourse.bacc as _bacc
    from concourse import mybir as _mybir
    from concourse.bass_utils import run_bass_kernel_spmd as _run

    f = {k: _np.asarray(v) for k, v in inputs.items()}
    tables = [f[n] for n in TABLES]
    offsets = _np.concatenate([[0], _np.cumsum([x.shape[0] for x in tables])[:-1]]).astype(_np.int32)
    row = _np.arange(HALF * NF).reshape(NCH, P).T
    rb, rn = row // NF, row % NF
    lookups = f["ids"].reshape(NT, 2, NCH, P).transpose(3, 0, 2, 1)
    starts = _np.broadcast_to(offsets[rn][:, None, :, None], (P, NT, NCH, 2))

    def rep(v):
        return _np.broadcast_to(v.reshape(1, -1), (P, v.size))

    wsi = f["L0_rec_Wsi"]
    pick = _np.arange(SW)[None, None, :] == (rb - _np.array([b for b, _ in ROWS_OF])[None, :])[:, :, None]
    block = _np.zeros((P, P), _np.float32)
    block[:D, :D] = block[D:, D:] = 1.0 / E
    i_of = _np.arange(P) % PR
    j_of = 4 * _np.arange(NG)[None, :] + _np.arange(P)[:, None] // PR
    gsi, bsi = f["L0_rec_gsi"], f["L0_rec_bsi"]
    one, zero = _np.ones((), gsi.dtype), _np.zeros((), gsi.dtype)
    mask9 = _np.zeros((P, 6), _np.float32)
    for r in range(9):
        mask9[r, r // 3] = mask9[r, 3 + r % 3] = 1.0
    cols = {
        "ident": _np.eye(P), "block": block,
        "wst": _np.concatenate([f["L0_rec_Ws"].T] * 2, 0),
        "wssel": wsi.T[rn].reshape(P, -1), "selmask": pick.reshape(P, -1),
        "eps": _np.full((P, 1), EPS),
        "gsrep": rep(f["L0_rec_gs"]), "bsrep": rep(f["L0_rec_bs"]), "wsirep": rep(wsi), "mask9": mask9,
        "gd": f["L0_rec_gd"][:, None], "bd": f["L0_rec_bd"][:, None],
        "gi": gsi[i_of][:, None], "bi": bsi[i_of][:, None],
        "gj": _np.where(j_of == 0, one, gsi[j_of - 1]), "bj": _np.where(j_of == 0, zero, bsi[j_of - 1]),
        "isi": i_of[:, None] == _np.arange(PR), "isj": (j_of[:, :, None] - 1 == _np.arange(PR)).reshape(P, -1),
        "isx": j_of == 0,
        "b1": f["b_top1"].reshape(-1, P).T, "b2": f["b_top2"].reshape(-1, P).T,
        "gl": f["L0_rec_gl"][:USED].reshape(KD, P).T, "bl": f["L0_rec_bl"][:USED].reshape(KD, P).T,
        "w3": f["W_top3"].reshape(-1, P).T,
    }

    def packed(pack):
        out = _np.zeros((P, sum(n for _, n in pack)), _np.float32)
        at = 0
        for name, n in pack:
            out[:, at:at + n] = cols[name]
            at += n
        return out

    tri = (i_of[:, None] + 1) * i_of[:, None] // 2 + j_of
    wl = _np.where((j_of <= i_of[:, None])[:, :, None], f["L0_rec_Wl"].T[_np.where(j_of <= i_of[:, None], tri, 0)], zero)
    w1 = _np.concatenate([f["W_top1"][:USED], f["W_top1"][MAXD:]], 0)
    arrays = {
        "table": _np.concatenate(tables, 0),
        "lookups": lookups, "starts": starts,
        "pack_a": packed(PACK_A), "pack_b": packed(PACK_B),
        "wdt": f["L0_rec_Wd"].T.reshape(KR, P, E).transpose(1, 0, 2),
        "denset": f["r_dense_t"].T.reshape(KR, P, B).transpose(1, 0, 2),
        "wlt": wl,
        "w1": w1.reshape(KW, P, H1).transpose(1, 0, 2),
        "w2": f["W_top2"].reshape(H1 // P, P, H2).transpose(1, 0, 2),
    }
    arrays = {k: _np.ascontiguousarray(v) for k, v in arrays.items()}
    nc = _bacc.Bacc("TRN2", target_bir_lowering=False, num_devices=1)
    args = {k: nc.dram_tensor(k, v.shape, _mybir.dt.from_np(v.dtype), kind="ExternalInput").ap()
            for k, v in arrays.items()}
    out = nc.dram_tensor("out", (1, B), _mybir.dt.float32, kind="ExternalOutput").ap()
    build(nc, out=out, **args)
    r = _run(nc, [arrays], core_ids=[0])
    return _np.asarray(r.results[0]["out"]).reshape(B, 1)
```

```python
from contextlib import ExitStack

import concourse.bass as bass
from concourse import mybir

F32 = mybir.dt.float32
BF16 = mybir.dt.bfloat16
F16 = mybir.dt.float16
I32 = mybir.dt.int32
ALU = mybir.AluOpType
ACT = mybir.ActivationFunctionType
AX = mybir.AxisListType

P = 128
B = 512
NF = 26
D = 64
E = 128
PR = 32
DD = 256
MAXD = 512
USED = 384
H1 = 512
H2 = 256
EPS = 1e-5

TILE = 128
NT = B // TILE
HALF = TILE // 2
NCH = HALF * NF // P
UR = 16
UPT = HALF // UR
NU = NT * UPT
CHUNKS = [range(0 if m == 0 else (UR * m * NF - 1) // P + 1, (UR * (m + 1) * NF - 1) // P + 1)
          for m in range(UPT)]
ROWS_OF = [(P * c // NF, (P * c + P - 1) // NF) for c in range(NCH)]
SW = 6
YC = 2 + PR
GC = PR + 1
NG = PR // 4
NQ = 4
FLAT_PARTS = 4
GP = NG // FLAT_PARTS
GSL = 2 * UR // 4
KD = USED // P
KR = DD // P
KW = KD + KR
KH = H1 // P

PACK_A = [("ident", P), ("block", P), ("wst", E), ("wssel", NCH * PR), ("selmask", NCH * SW), ("eps", 1)]
PACK_B = [("gsrep", E), ("one", 1), ("wsirep", PR * NF), ("mask9", 6), ("gd", 1), ("bd", 1),
          ("gi", 1), ("bi", 1), ("gj", NG), ("bj", NG), ("isi", PR), ("isj", NG * PR), ("isx", NG),
          ("b1", H1 // P), ("b2", H2 // P), ("gl", KD), ("bl", KD), ("w3", H2 // P)]


def columns(pack):
    at, out = 0, {}
    for name, n in pack:
        out[name] = (at, at + n)
        at += n
    return out, at


COL_A, NA = columns(PACK_A)
COL_B, NB = columns(PACK_B)


def build(nc, table, lookups, starts, pack_a, pack_b, bsrep, zxinit, zeros, wdt, denset, wlt, w1, w2, out):
    with ExitStack() as ctx:
        def sb(name, shape, dt=F32):
            return ctx.enter_context(nc.sbuf_tensor(name, shape, dt))

        def ps(name, shape):
            return ctx.enter_context(nc.psum_tensor(name, shape, F32))

        def sem(name):
            return ctx.enter_context(nc.semaphore(name))

        a_sb = sb("a_sb", [P, NA])
        b_sb = sb("b_sb", [P, NB])

        def pa(name, rows=slice(0, P)):
            lo, hi = COL_A[name]
            return a_sb[rows, lo:hi]

        def pb(name, rows=slice(0, P)):
            lo, hi = COL_B[name]
            return b_sb[rows, lo:hi]

        rel = sb("rel", [P, NT, NCH, 2], I32)
        first = sb("first", [P, NT, NCH, 2], I32)
        idx = sb("idx", [P, NT * NCH * 2], I32)
        emb = sb("emb", [P, NT * NCH * 2, D])
        prod = sb("prod", [P, 8 * D])
        var = sb("var", [P, NT * NCH * 2])
        std = sb("std", [P, NT * NCH * 2])
        inv = sb("inv", [P, NT * NCH * 2])
        embt = [sb(f"embt{i}", [P, 4 * P]) for i in range(2)]
        wt = [sb(f"wt{i}", [P, 2, UR * PR], F16) for i in range(2)]
        sq = sb("sq", [P, 2 * UR * PR])
        vary = [sb(f"vary{i}", [P, 2 * UR]) for i in range(2)]
        stdy = [sb(f"stdy{i}", [P, 2 * UR]) for i in range(2)]
        invy = [sb(f"invy{i}", [P, 2 * UR]) for i in range(2)]
        tt = sb("tt", [P, B, YC])
        zs = [sb(f"zs{i}", [P, NG, TILE]) for i in range(2)]
        zx = sb("zx", [P, B])
        wl = sb("wl", [P, NG, MAXD])
        wx = sb("wx", [P, MAXD])
        mx = sb("mx", [P, NG, 96])
        mxt = sb("mxt", [P, NG, PR])
        w1s = sb("w1s", [P, KW, H1])
        w2s = sb("w2s", [P, H1 // P, H2])
        wds = sb("wds", [P, KR, E])
        dts = sb("dts", [P, KR, B])
        wm = sb("wm", [P, NCH])
        wsel = sb("wsel", [P, NCH, PR])
        sel = sb("sel", [P, NCH, SW, PR])
        mean1 = sb("mean1", [P, 1])
        wsc = sb("wsc", [P, E])
        wsce = sb("wsce", [P, P])
        g2 = sb("g2", [P, P])
        wvf = sb("wvf", [P, E])
        wvh = sb("wvh", [P, E], F16)
        wvl = sb("wvl", [P, E], F16)
        rest = sb("rest", [P, E + PR])
        part = [sb(f"part{i}", [P, E + PR], BF16) for i in range(3)]
        bs9 = sb("bs9", [P, E], BF16)
        ws9 = sb("ws9", [P, PR], BF16)
        ws9r = sb("ws9r", [P, UR, PR], BF16)
        wsum = sb("wsum", [P, PR])
        wmean = sb("wmean", [P, 1])
        xst = sb("xst", [P, NT, 6])
        xmv = sb("xmv", [P, NT, 2])
        xstd = sb("xstd", [P, NT])
        xinv = sb("xinv", [P, NT])
        xn = sb("xn", [P, NT, E])
        gibj = sb("gibj", [P, NG])
        gjbi = sb("gjbi", [P, NG])
        gij = sb("gij", [P, NG])
        b1e = sb("b1e", [P, H1 // P])
        ost = sb("ost", [P, 6])
        omv = sb("omv", [P, 2])
        ostd = sb("ostd", [P, 1])
        oinv = sb("oinv", [P, 1])
        onmr = sb("onmr", [P, 1])
        zn = sb("zn", [P, USED])
        znt = sb("znt", [P, KD, TILE])
        h1 = sb("h1", [P, H1 // P, TILE])
        h2 = sb("h2", [P, H2 // P, TILE])
        yrow = sb("yrow", [1, B])

        pq = ps("pq", [P, 4 * P])
        pw = [ps(f"pw{i}", [P, 512]) for i in range(2)]
        pv = ps("pv", [P, 2, 512])
        pg = ps("pg", [P, 2, 512])
        po = ps("po", [P, 512])

        ld_rel, ld_first, ld_a, ld_b, ld_x, ld_w1, ld_w2, ld_dt, ld_bs, ld_zx, ld_mx, ld_wx = (
            sem(n) for n in ("ld_rel", "ld_first", "ld_a", "ld_b", "ld_x", "ld_w1", "ld_w2", "ld_dt",
                              "ld_bs", "ld_zx", "ld_mx", "ld_wx"))
        ld_wl = [sem(f"ld_wl{i}") for i in range(2)]
        idx_ready = sem("idx_ready")
        gathered = [sem(f"gathered{u}") for u in range(NU)]
        setup_v = sem("setup_v")
        setup_pe = sem("setup_pe")
        setup_a = sem("setup_a")
        tr_done, embt_ready, q_done, prod_ready, var_ready, std_ready, inv_ready, scaled = (
            sem(n) for n in ("tr_done", "embt_ready", "q_done", "prod_ready", "var_ready", "std_ready",
                             "inv_ready", "scaled"))
        contracted, hi_ready, wt_ready, v_done, sq_ready, vary_ready, stdy_ready, invy_ready, t_ready = (
            sem(n) for n in ("contracted", "hi_ready", "wt_ready", "v_done", "sq_ready", "vary_ready", "stdy_ready",
                             "invy_ready", "t_ready"))
        gram_done, z_ready = sem("gram_done"), sem("z_ready")
        o_done, ost_ready, omv_ready, ostd_ready, oinv_ready, onmr_ready, zn_ready, znt_done, znt_ready = (
            sem(n) for n in ("o_done", "ost_ready", "omv_ready", "ostd_ready", "oinv_ready", "onmr_ready",
                             "zn_ready", "znt_done", "znt_ready"))
        h1_done, h1_ready, h2_done, h2_ready, y_done, y_ready = (
            sem(n) for n in ("h1_done", "h1_ready", "h2_done", "h2_ready", "y_done", "y_ready"))
        stored = sem("stored")

        def kof(u):
            t, m = divmod(u, UPT)
            return (t * NCH + CHUNKS[m][0]) * 2, 2 * len(CHUNKS[m])

        def h1_sums(t, o):
            if t == NT - 1:
                return (pq[:, 0:P], pw[0][:, 0:P], pw[1][:, 0:P], pv[:, 0, 0:P])[o]
            return po[:, o * P:(o + 1) * P]

        block = ctx.enter_context(nc.Block())

        @block.sync
        def _(sp):
            sp.dma_start(rel[:, :, :, :], lookups).then_inc(ld_rel, 16)
            sp.dma_start(first[:, :, :, :], starts).then_inc(ld_first, 16)
            sp.dma_start(a_sb[:, :], pack_a).then_inc(ld_a, 16)
            sp.dma_start(b_sb[:, :], pack_b).then_inc(ld_b, 16)
            sp.dma_start(rest[:, 0:E], bsrep).then_inc(ld_bs, 16)
            sp.dma_start(wds[:, :, :], wdt).then_inc(ld_x, 16)
            sp.dma_start(dts[:, :, :], denset).then_inc(ld_dt, 16)
            sp.dma_start(zx[:, :], zxinit).then_inc(ld_zx, 16)
            sp.dma_start(mx[:, :, PR:], zeros[:, 0:NG * (96 - PR)].rearrange("p (g q) -> p g q", g=NG)).then_inc(ld_mx, 16)
            sp.dma_start(wx[96:P, :], zeros[96:P, :]).then_inc(ld_wx, 16)
            sp.wait_ge(gathered[0], 16 * kof(0)[1])
            for i in range(2):
                half = slice(i * NG // 2, (i + 1) * NG // 2)
                sp.dma_start(wl[:, half, :], wlt[:, half, :]).then_inc(ld_wl[i], 16)
            sp.wait_ge(gathered[1], 16 * kof(1)[1])
            sp.dma_start(w1s[:, :, :], w1).then_inc(ld_w1, 16)
            sp.wait_ge(gathered[2], 16 * kof(2)[1])
            sp.dma_start(w2s[:, :, :], w2).then_inc(ld_w2, 16)
            sp.wait_ge(y_ready, NT)
            sp.dma_start(out, yrow[:, :]).then_inc(stored, 16)
            sp.wait_ge(stored, 16)

        @block.gpsimd
        def _(pool):
            pool.wait_ge(ld_rel, 16)
            pool.wait_ge(ld_first, 16)
            pool.tensor_tensor(idx[:, :], rel[:, :, :, :].rearrange("p t c s -> p (t c s)"),
                               first[:, :, :, :].rearrange("p t c s -> p (t c s)"), ALU.add).then_inc(idx_ready, 1)
            pool.wait_ge(idx_ready, 1)
            for u in range(NU):
                k0, nk = kof(u)
                for k in range(k0, k0 + nk):
                    pool.indirect_dma_start(emb[:, k, :], None, table,
                                            bass.IndirectOffsetOnAxis(ap=idx[:, k:k + 1], axis=0)
                                            ).then_inc(gathered[u], 16)

        def numbered(*names):
            return {n: i + 1 for i, n in enumerate(names)}

        V = numbered(
            "wsum1", "wmean1", "wsc", "wvf", "wvh", "wvl", "wsum", "wsumsum", "wmean",
            "rest0", "g2", "selsum", "selmean", "selc", "sel", "xst", "xmv", "xinv", "xn",
            "part0", "left0", "part1", "left1", "part2", "xt", "gibj", "gjbi", "gij",
            "mxi", "mxj", "mxs", "mxx", "mx", "bs9_0", "ws9_0", "bs9_1", "ws9_1", "bs9_2",
            "ws9_2", "ws9r", "b1e")
        PES = numbered(
            "wsct", "g", "x", "xt", "xs", "wx", "b1")
        AS = numbered(
            "table", "wsce", "ones", "xstd", "xs", "wx", "wls0", "wls1", "wls2", "wls3",
            "w1s")
        @block.tensor
        def _(pe):
            def transposes(u):
                k0, nk = kof(u)
                pe.wait_ge(gathered[u], 16 * nk)
                if u:
                    pe.wait_ge(prod_ready, u)
                else:
                    pe.wait_ge(ld_a, 16)
                for c in range(nk // 2):
                    mm = pe.transpose(pq[:, c * P:(c + 1) * P],
                                      emb[:, k0 + 2 * c:k0 + 2 * c + 2, :].rearrange("p s d -> p (s d)"), pa("ident"))
                mm.then_inc(tr_done, 1)

            def quadratic(u):
                pe.wait_ge(embt_ready, u + 1)
                _, nk = kof(u)
                for c in range(nk // 2):
                    mm = pe.matmul(pq[:, c * P:(c + 1) * P], embt[u % 2][:, c * P:(c + 1) * P], g2[:, :],
                                   start=True, stop=True)
                mm.then_inc(q_done, 1)

            def contract(u):
                t, m = divmod(u, UPT)
                pe.wait_ge(scaled, u + 1)
                if u == 0:
                    pe.wait_ge(setup_v, V["sel"])
                if u:
                    pe.wait_ge(wt_ready, u)
                for c in CHUNKS[m]:
                    b0, b1 = ROWS_OF[c]
                    k = (t * NCH + c) * 2
                    lhs = emb[:, k:k + 2, :].rearrange("p s d -> p (s d)")
                    for mm_ in (m, m + 1):
                        lo, hi = max(b0, UR * mm_), min(b1 + 1, UR * (mm_ + 1))
                        if lo >= hi:
                            continue
                        mm = pe.matmul(pw[(t * UPT + mm_) % 2][:, (lo - UR * mm_) * PR:(hi - UR * mm_) * PR],
                                       lhs, sel[:, c, lo - b0:hi - b0, :].rearrange("p j q -> p (j q)"),
                                       start=(mm_ > m or (m == 0 and c == 0)), stop=True, skip_group_check=True)
                mm.then_inc(contracted, 1)

            def expand(u):
                pe.wait_ge(wt_ready, u + 1)
                if u == 0:
                    pe.wait_ge(setup_v, V["ws9r"])
                if u:
                    pe.wait_ge(t_ready, u)
                for s in range(2):
                    pe.matmul(pv[:, s, :], wvh[:, :], wt[u % 2][:, s, :], start=True, stop=False)
                    pe.matmul(pv[:, s, :], wvl[:, :], wt[u % 2][:, s, :], start=False, stop=False)
                    mm = pe.matmul(pv[:, s, :], bs9[:, :], ws9r[:, :, :].rearrange("p b q -> p (b q)"),
                                   start=False, stop=True)
                mm.then_inc(v_done, 1)

            def gram(u):
                t, m = divmod(u, UPT)
                pe.wait_ge(t_ready, u + 1)
                if u == 0:
                    pe.wait_ge(setup_v, V["xt"])
                    pe.wait_ge(setup_a, AS["ones"])
                if u >= 2 and u % 2 == 0:
                    pe.wait_ge(z_ready, NQ * (u // 2))
                for s in range(2):
                    for j in range(UR):
                        b = t * TILE + s * HALF + UR * m + j
                        q, slot = j % 4, (m % 2) * 4 + j // 4
                        mm = pe.matmul(pg[32 * q:32 * q + 32, s, slot * GC:(slot + 1) * GC],
                                       tt[:, b, 2:YC], tt[:, b, 0:GC], start=True, stop=True)
                mm.then_inc(gram_done, 1)

            def flat_linear(t, part):
                if part == 0:
                    pe.wait_ge(z_ready, NQ * (2 * t + 2))
                    if t:
                        pe.wait_ge(y_ready, t)
                    else:
                        pe.wait_ge(setup_v, V["b1e"])
                        pe.wait_ge(setup_a, AS["wls3"])
                for g in range(GP * part, GP * part + GP):
                    pe.matmul(po[:, :], zs[t % 2][:, g, :], wl[:, g, :], start=(g == 0), stop=False)
                if part == FLAT_PARTS - 1:
                    pe.matmul(po[:, :], zx[:, t * TILE:(t + 1) * TILE], wx[:, :], start=False, stop=True
                              ).then_inc(o_done, 1)

            def z_transposes(t):
                pe.wait_ge(zn_ready, t + 1)
                for c in range(KD):
                    mm = pe.transpose(po[:, c * P:(c + 1) * P], zn[:, c * P:(c + 1) * P], pa("ident"))
                mm.then_inc(znt_done, 1)

            def top1_dense(t):
                if t == NT - 1:
                    pe.wait_ge(prod_ready, NU)
                    pe.wait_ge(wt_ready, NU)
                    pe.wait_ge(t_ready, NU)
                else:
                    pe.wait_ge(znt_ready, t + 1)
                if t == 0:
                    pe.wait_ge(setup_a, AS["w1s"])
                for o in range(H1 // P):
                    for c in range(KD, KW):
                        pe.matmul(h1_sums(t, o), w1s[:, c, o * P:(o + 1) * P],
                                  dts[:, c - KD, t * TILE:(t + 1) * TILE], start=(c == KD and (o == 0 or t == NT - 1)), stop=False,
                                  skip_group_check=True)

            def top1(t, o):
                if o == 0:
                    pe.wait_ge(znt_ready, t + 1)
                for c in range(KD):
                    mm = pe.matmul(h1_sums(t, o), w1s[:, c, o * P:(o + 1) * P], znt[:, c, :],
                                   start=False, stop=(c == KD - 1), skip_group_check=True)
                mm.then_inc(h1_done, 1)

            def top2(t, c):
                pe.wait_ge(h1_ready, KH * t + (c + 1 if t == NT - 1 else KH))
                if t == 0 and c == 0:
                    pe.wait_ge(ld_w2, 16)
                for o in range(H2 // P):
                    mm = pe.matmul(po[:, o * P:(o + 1) * P], w2s[:, c, o * P:(o + 1) * P], h1[:, c, :],
                                   start=(c == 0 and o == 0), stop=(c == KH - 1), skip_group_check=True)
                if c == KH - 1:
                    mm.then_inc(h2_done, 1)

            def top3(t):
                pe.wait_ge(h2_ready, t + 1)
                for c in range(H2 // P):
                    mm = pe.matmul(po[0:1, 0:P], pb("w3")[:, c:c + 1], h2[:, c, :],
                                   start=(c == 0), stop=(c == H2 // P - 1))
                mm.then_inc(y_done, 1)

            def transpose_ws():
                pe.wait_ge(ld_a, 16)
                pe.wait_ge(setup_v, V["wsc"])
                pe.transpose(po[:, 0:P], wsc[:, :], pa("ident")).then_inc(setup_pe, 1)

            def g_product():
                pe.wait_ge(setup_a, AS["wsce"])
                pe.matmul(po[:, 0:P], wsce[:, :], wsce[:, :], start=True, stop=True).then_inc(setup_pe, 1)

            def x_product():
                pe.wait_ge(setup_v, V["g2"])
                pe.wait_ge(ld_x, 16)
                pe.wait_ge(ld_dt, 16)
                for t in range(NT):
                    for c in range(KR):
                        mm = pe.matmul(po[:, t * E:(t + 1) * E], dts[:, c, t * TILE:(t + 1) * TILE], wds[:, c, :],
                                       start=(c == 0), stop=(c == KR - 1))
                mm.then_inc(setup_pe, 1)

            def x_transposes():
                pe.wait_ge(setup_v, V["xn"])
                for t in range(NT):
                    mm = pe.transpose(po[:, t * TILE:(t + 1) * TILE], xn[:, t, :], pa("ident"))
                mm.then_inc(setup_pe, 1)

            def x_sums():
                pe.wait_ge(setup_v, V["xt"])
                pe.wait_ge(setup_a, AS["ones"])
                pe.matmul(po[32:33, 0:B], tt[:, 0, 0:1], tt[:, :, 1], start=True, stop=True).then_inc(setup_pe, 1)

            def zx_weights(part):
                if part == 0:
                    pe.wait_ge(setup_a, AS["xs"])
                    pe.wait_ge(setup_v, V["mx"])
                    pe.wait_ge(ld_mx, 16)
                    for part_landed in ld_wl:
                        pe.wait_ge(part_landed, 16)
                for g in range(GP * part, GP * part + GP):
                    mm = pe.matmul(po[0:96, :], mx[:, g, :], wl[:, g, :], start=(g == 0), stop=(g == NG - 1))
                if part == FLAT_PARTS - 1:
                    mm.then_inc(setup_pe, 1)

            def bl_product():
                pe.wait_ge(setup_a, AS["wx"])
                pe.wait_ge(ld_w1, 16)
                for o in range(H1 // P):
                    for c in range(KD):
                        mm = pe.matmul(po[:, o:o + 1], w1s[:, c, o * P:(o + 1) * P], pb("bl")[:, c:c + 1],
                                       start=(c == 0), stop=(c == KD - 1))
                mm.then_inc(setup_pe, 1)

            transpose_ws()
            g_product()
            x_product()
            x_transposes()
            x_sums()
            for i in range(7, 31):
                if (i - 16) % UPT == 0 and 0 <= i - 16 < NU:
                    z_transposes((i - 16) // UPT)
                if (i - 18) % UPT == 0 and 0 <= i - 18 < NU:
                    top2((i - 18) // UPT, 0)
                if (i - 17) % UPT == 0 and 0 <= i - 17 < NU:
                    top1((i - 17) // UPT, 1)
                    top1((i - 17) // UPT, 2)
                if (i - 15) % UPT == 0 and 0 <= i - 15 < NU:
                    flat_linear((i - 15) // UPT, 1)
                    flat_linear((i - 15) // UPT, 2)
                if 0 <= i - 7 < NU:
                    transposes(i - 7)
                if (i - 17) % UPT == 0 and 0 <= i - 17 < NU:
                    top1((i - 17) // UPT, 3)
                if (i - 15) % UPT == 0 and 0 <= i - 15 < NU:
                    flat_linear((i - 15) // UPT, 3)
                if i == 7:
                    zx_weights(0)
                if 0 <= i - 11 < NU:
                    gram(i - 11)
                if (i - 18) % UPT == 0 and 0 <= i - 18 < NU:
                    top2((i - 18) // UPT, 1)
                if i == 8:
                    zx_weights(2)
                if i == 9:
                    zx_weights(3)
                if 0 <= i - 7 < NU:
                    quadratic(i - 7)
                if (i - 18) % UPT == 0 and 0 <= i - 18 < NU:
                    top2((i - 18) // UPT, 2)
                if i == 10:
                    bl_product()
                if (i - 16) % UPT == 0 and 0 <= i - 16 < NU:
                    top1_dense((i - 16) // UPT)
                if i == 7:
                    zx_weights(1)
                if (i - 18) % UPT == 0 and 0 <= i - 18 < NU:
                    top2((i - 18) // UPT, 3)
                if 0 <= i - 8 < NU:
                    contract(i - 8)
                if (i - 18) % UPT == 0 and 0 <= i - 18 < NU:
                    top3((i - 18) // UPT)
                if (i - 16) % UPT == 0 and 0 <= i - 16 < NU:
                    top1((i - 16) // UPT, 0)
                if 0 <= i - 9 < NU:
                    expand(i - 9)
                if (i - 14) % UPT == 0 and 0 <= i - 14 < NU:
                    flat_linear((i - 14) // UPT, 0)

        def z_parts(h, q):
            t = h // 2
            b0 = 32 * (h % 2) + q
            src = pg[32 * q:32 * q + 32, :, 0:GSL * GC].rearrange("p s (l c) -> p s l c", c=GC)
            dst = zs[t % 2][:, :, :].rearrange("p g (s r) -> p s r g", s=2)
            return [(src[:, :, :, 1 + j:GC:4], dst[32 * j:32 * j + 32, :, b0:b0 + 29:4, :]) for j in range(4)]

        def zx_part(h, q):
            t = h // 2
            b0 = 32 * (h % 2) + q
            src = pg[32 * q:32 * q + 32, :, 0:GSL * GC].rearrange("p s (l c) -> p s l c", c=GC)[:, :, :, 0]
            dst = zx[0:32, t * TILE:(t + 1) * TILE].rearrange("p (s r) -> p s r", s=2)[:, :, b0:b0 + 29:4]
            return src, dst

        @block.scalar
        def _(act):
            def embt_copy(u):
                act.wait_ge(tr_done, u + 1)
                if u >= 2:
                    act.wait_ge(q_done, u - 1)
                _, nk = kof(u)
                n = nk // 2 * P
                act.activation(embt[u % 2][:, 0:n], pq[:, 0:n], ACT.Copy).then_inc(embt_ready, 1)

            def std_rows(u):
                k0, nk = kof(u)
                act.wait_ge(var_ready, u + 1)
                act.activation(std[:, k0:k0 + nk], var[:, k0:k0 + nk], ACT.Sqrt, bias=pa("eps")).then_inc(std_ready, 1)

            def wt_hi(u):
                act.wait_ge(contracted, u + 1)
                if u >= 2:
                    act.wait_ge(v_done, u - 1)
                for s in range(2):
                    here = slice(D * s, D * s + D)
                    act.activation(wt[u % 2][here, s, :], pw[u % 2][here, :], ACT.Copy).then_inc(hi_ready, 1)

            def squares(u):
                act.wait_ge(v_done, u + 1)
                if u:
                    act.wait_ge(vary_ready, u)
                act.activation(sq[:, :], pv[:, :, :].rearrange("p s c -> p (s c)"), ACT.Square,
                               scale=float(PR) ** -0.5).then_inc(sq_ready, 1)

            def std_y(u):
                act.wait_ge(vary_ready, u + 1)
                if u >= 2:
                    act.wait_ge(invy_ready, u - 1)
                act.activation(stdy[u % 2][:, :], vary[u % 2][:, :], ACT.Sqrt, bias=pa("eps")).then_inc(stdy_ready, 1)

            def z_copies(h, q):
                act.wait_ge(gram_done, 2 * h + 2)
                if h % 2 == 0 and h >= 4:
                    act.wait_ge(o_done, h // 2 - 1)
                for src, dst in z_parts(h, q):
                    act.activation(dst, src, ACT.Copy)
                src, dst = zx_part(h, q)
                act.activation(dst, src, ACT.Copy).then_inc(z_ready, 1)

            def std_o(t):
                act.wait_ge(omv_ready, t + 1)
                act.activation(ostd[:, :], omv[:, 1:2], ACT.Sqrt, bias=pa("eps")).then_inc(ostd_ready, 1)

            def normalise(t):
                act.wait_ge(onmr_ready, t + 1)
                act.activation(zn[:, :], po[:, 0:USED], ACT.Identity, bias=onmr[:, :], scale=oinv[:, :]
                               ).then_inc(zn_ready, 1)

            def relu1(t, o):
                act.wait_ge(h1_done, KH * t + (o + 1 if t == NT - 1 else KH))
                act.activation(h1[:, o, :], h1_sums(t, o), ACT.Relu, bias=b1e[:, o:o + 1]
                               ).then_inc(h1_ready, 1)

            def relu2(t):
                act.wait_ge(h2_done, t + 1)
                for o in range(H2 // P):
                    last = act.activation(h2[:, o, :], po[:, o * P:(o + 1) * P], ACT.Relu,
                                          bias=pb("b2")[:, o:o + 1])
                last.then_inc(h2_ready, 1)

            def load_table():
                act.wait_ge(ld_a, 16)
                act.activation(ostd[:, :], pa("eps"), ACT.Sqrt).then_inc(setup_a, 1)

            def wsce_copy():
                act.wait_ge(setup_pe, PES["wsct"])
                act.activation(wsce[:, :], po[:, 0:P], ACT.Copy).then_inc(setup_a, 1)

            def ones():
                act.wait_ge(ld_b, 16)
                act.activation(tt[:, :, 0], pb("one").broadcast_to([P, B]), ACT.Copy).then_inc(setup_a, 1)

            def std_x():
                act.wait_ge(setup_v, V["xmv"])
                act.activation(xstd[:, :], xmv[:, :, 1], ACT.Sqrt, bias=pa("eps")).then_inc(setup_a, 1)

            def x_sums_copy():
                act.wait_ge(setup_pe, PES["xs"])
                act.wait_ge(ld_zx, 16)
                act.activation(zx[32:33, :], po[32:33, 0:B], ACT.Copy).then_inc(setup_a, 1)

            def zx_weights_copy():
                act.wait_ge(setup_pe, PES["wx"])
                act.activation(wx[0:96, :], po[0:96, :], ACT.Copy).then_inc(setup_a, 1)

            def scale_wl(part):
                act.wait_ge(setup_pe, PES["wx"])
                act.wait_ge(setup_v, V["gij"])
                for g in range(GP * part, GP * part + GP):
                    last = act.activation(wl[:, g, :], wl[:, g, :], ACT.Copy, scale=gij[:, g:g + 1])
                last.then_inc(setup_a, 1)

            def scale_w1():
                act.wait_ge(setup_pe, PES["b1"])
                for c in range(KD):
                    last = act.activation(w1s[:, c, :], w1s[:, c, :], ACT.Copy, scale=pb("gl")[:, c:c + 1])
                last.then_inc(setup_a, 1)

            load_table()
            wsce_copy()
            ones()
            std_x()
            x_sums_copy()
            for i in range(7, 32):
                if 0 <= i - 11 < NU:
                    std_y(i - 11)
                if i == 16:
                    scale_w1()
                if i == 11:
                    scale_wl(0)
                if (i - 13) % 2 == 0 and 0 <= i - 13 < NU:
                    z_copies((i - 13) // 2, 0)
                if i == 12:
                    scale_wl(3)
                if (i - 13) % 2 == 0 and 0 <= i - 13 < NU:
                    z_copies((i - 13) // 2, 1)
                if (i - 16) % UPT == 0 and 0 <= i - 16 < NU:
                    std_o((i - 16) // UPT)
                if (i - 19) % UPT == 0 and 0 <= i - 19 < NU:
                    relu2((i - 19) // UPT)
                if (i - 13) % 2 == 0 and 0 <= i - 13 < NU:
                    z_copies((i - 13) // 2, 2)
                if (i - 18) % UPT == 0 and 0 <= i - 18 < NU:
                    relu1((i - 18) // UPT, 1)
                if i == 10:
                    zx_weights_copy()
                if (i - 18) % UPT == 0 and 0 <= i - 18 < NU:
                    relu1((i - 18) // UPT, 2)
                    relu1((i - 18) // UPT, 3)
                if (i - 13) % 2 == 0 and 0 <= i - 13 < NU:
                    z_copies((i - 13) // 2, 3)
                if i == 11:
                    scale_wl(1)
                if (i - 16) % UPT == 0 and 0 <= i - 16 < NU:
                    normalise((i - 16) // UPT)
                if 0 <= i - 9 < NU:
                    wt_hi(i - 9)
                if 0 <= i - 8 < NU:
                    std_rows(i - 8)
                if 0 <= i - 10 < NU:
                    squares(i - 10)
                if i == 11:
                    scale_wl(2)
                if 0 <= i - 7 < NU:
                    embt_copy(i - 7)
                if (i - 17) % UPT == 0 and 0 <= i - 17 < NU:
                    relu1((i - 17) // UPT, 0)

        @block.vector
        def _(dve):
            def products(u):
                k0, nk = kof(u)
                dve.wait_ge(q_done, u + 1)
                if u:
                    dve.wait_ge(var_ready, u)
                dve.tensor_tensor(prod[:, 0:nk * D], pq[:, 0:nk * D],
                                  emb[:, k0:k0 + nk, :].rearrange("p k d -> p (k d)"), ALU.mult
                                  ).then_inc(prod_ready, 1)
                dve.wait_ge(prod_ready, u + 1)
                dve.tensor_reduce(var[:, k0:k0 + nk], prod[:, 0:nk * D].rearrange("p (k d) -> p k d", d=D),
                                  AX.X, ALU.add).then_inc(var_ready, 1)

            def scale_rows(u):
                k0, nk = kof(u)
                dve.wait_ge(std_ready, u + 1)
                dve.reciprocal(inv[:, k0:k0 + nk], std[:, k0:k0 + nk]).then_inc(inv_ready, 1)
                dve.wait_ge(inv_ready, u + 1)
                dve.tensor_tensor(emb[:, k0:k0 + nk, :], emb[:, k0:k0 + nk, :],
                                  inv[:, k0:k0 + nk].unsqueeze(2).broadcast_to([P, nk, D]), ALU.mult
                                  ).then_inc(scaled, 1)

            def wt_lo(u):
                for s in range(2):
                    dve.wait_ge(hi_ready, 2 * u + s + 1)
                    here, other = slice(D * s, D * s + D), slice(D * (1 - s), D * (1 - s) + D)
                    last = dve.tensor_tensor(wt[u % 2][other, s, :], pw[u % 2][here, :], wt[u % 2][here, s, :],
                                             ALU.subtract)
                last.then_inc(wt_ready, 1)

            def var_y(u):
                dve.wait_ge(sq_ready, u + 1)
                if u >= 2:
                    dve.wait_ge(stdy_ready, u - 1)
                dve.tensor_reduce(vary[u % 2][:, :], sq[:, :].rearrange("p (b q) -> p b q", q=PR),
                                  AX.X, ALU.add).then_inc(vary_ready, 1)

            def scale_y(u):
                t, m = divmod(u, UPT)
                dve.wait_ge(stdy_ready, u + 1)
                dve.reciprocal(invy[u % 2][:, :], stdy[u % 2][:, :]).then_inc(invy_ready, 1)
                dve.wait_ge(invy_ready, u + 1)
                for s in range(2):
                    b = t * TILE + s * HALF + UR * m
                    last = dve.tensor_tensor(
                        tt[:, b:b + UR, 2:YC], pv[:, s, :].rearrange("p (b q) -> p b q", q=PR),
                        invy[u % 2][:, s * UR:(s + 1) * UR].unsqueeze(2).broadcast_to([P, UR, PR]), ALU.mult)
                last.then_inc(t_ready, 1)

            def stats(t):
                dve.wait_ge(o_done, t + 1)
                dve.bn_stats(ost[:, :], po[:, :]).then_inc(ost_ready, 1)
                dve.wait_ge(ost_ready, t + 1)
                dve.bn_aggr(omv[:, :], ost[:, :]).then_inc(omv_ready, 1)

            def shift_o(t):
                dve.wait_ge(ostd_ready, t + 1)
                dve.reciprocal(oinv[:, :], ostd[:, :]).then_inc(oinv_ready, 1)
                dve.wait_ge(oinv_ready, t + 1)
                dve.scalar_tensor_tensor(out=onmr[:, :], in0=omv[:, 0:1], scalar=-1.0, in1=oinv[:, :],
                                         op0=ALU.mult, op1=ALU.mult).then_inc(onmr_ready, 1)

            def znt_copy(t):
                dve.wait_ge(znt_done, t + 1)
                if t:
                    dve.wait_ge(h1_done, KH * t)
                dve.tensor_copy(znt[:, :, :].rearrange("p c b -> p (c b)"), po[:, 0:USED]).then_inc(znt_ready, 1)

            def y_copy(t):
                dve.wait_ge(y_done, t + 1)
                dve.tensor_copy(yrow[:, t * TILE:(t + 1) * TILE], po[0:1, 0:P]).then_inc(y_ready, 1)

            def done(name, ins):
                ins.then_inc(setup_v, 1)
                dve.wait_ge(setup_v, V[name])

            def centre_ws():
                dve.wait_ge(ld_a, 16)
                done("wsum1", dve.tensor_reduce(mean1[:, :], pa("wst"), AX.X, ALU.add))
                done("wmean1", dve.tensor_scalar(mean1[:, :], mean1[:, :], 1.0 / E, None, ALU.mult))
                done("wsc", dve.tensor_scalar(wsc[:, :], pa("wst"), mean1[:, :], None, ALU.subtract))

            def centre_wsi():
                wssel = pa("wssel").rearrange("p (c q) -> p c q", q=PR)
                done("selsum", dve.tensor_reduce(wm[:, :], wssel, AX.X, ALU.add))
                done("selmean", dve.tensor_scalar(wm[:, :], wm[:, :], 1.0 / PR, None, ALU.mult))
                done("selc", dve.tensor_tensor(wsel[:, :, :], wssel,
                                               wm[:, :].unsqueeze(2).broadcast_to([P, NCH, PR]), ALU.subtract))

            def spread_wsi():
                done("sel", dve.tensor_tensor(
                    sel[:, :, :, :], wsel[:, :, :].unsqueeze(2).broadcast_to([P, NCH, SW, PR]),
                    pa("selmask").rearrange("p (c j) -> p c j", j=SW).unsqueeze(3).broadcast_to([P, NCH, SW, PR]),
                    ALU.mult))

            def g_blocks():
                dve.wait_ge(setup_pe, PES["g"])
                done("g2", dve.tensor_tensor(g2[:, :], po[:, 0:P], pa("block"), ALU.mult))

            def x_stats():
                dve.wait_ge(setup_pe, PES["x"])
                for t in range(NT):
                    last = dve.bn_stats(xst[:, t, :], po[:, t * E:(t + 1) * E])
                done("xst", last)
                for t in range(NT):
                    last = dve.bn_aggr(xmv[:, t, :], xst[:, t, :])
                done("xmv", last)

            def x_norm():
                dve.wait_ge(setup_a, AS["xstd"])
                done("xinv", dve.reciprocal(xinv[:, :], xstd[:, :]))
                for t in range(NT):
                    last = dve.tensor_scalar(xn[:, t, :], po[:, t * E:(t + 1) * E], xmv[:, t, 0:1],
                                             xinv[:, t:t + 1], ALU.subtract, ALU.mult)
                done("xn", last)

            def expand_weights():
                dve.wait_ge(ld_b, 16)
                done("wvf", dve.tensor_tensor(wvf[:, :], wsc[:, :], pb("gsrep"), ALU.mult))
                done("wvh", dve.tensor_copy(wvh[:, :], wvf[:, :]))
                done("wvl", dve.tensor_tensor(wvl[:, :], wvf[:, :], wvh[:, :], ALU.subtract))

            def wsi_sums():
                dve.wait_ge(ld_b, 16)
                done("wsum", dve.tensor_reduce(wsum[:, :], pb("wsirep").rearrange("p (q n) -> p q n", n=NF),
                                               AX.X, ALU.add))
                done("wsumsum", dve.tensor_reduce(wmean[:, :], wsum[:, :], AX.X, ALU.add))
                done("wmean", dve.tensor_scalar(wmean[:, :], wmean[:, :], 1.0 / PR, None, ALU.mult))
                done("rest0", dve.tensor_scalar(rest[:, E:E + PR], wsum[:, :], wmean[:, :], None, ALU.subtract))

            def split_bias():
                dve.wait_ge(ld_bs, 16)
                for i in range(3):
                    done(f"part{i}", dve.tensor_copy(part[i][:, :], rest[:, :]))
                    if i < 2:
                        done(f"left{i}", dve.tensor_tensor(rest[:, :], rest[:, :], part[i][:, :], ALU.subtract))

            def bias_products():
                m9 = pb("mask9")
                done("bs9_0", dve.tensor_scalar(bs9[:, :], part[0][:, 0:E], m9[:, 0:1], None, ALU.mult))
                done("ws9_0", dve.tensor_scalar(ws9[:, :], part[0][:, E:E + PR], m9[:, 3:4], None, ALU.mult))
                for i in (1, 2):
                    done(f"bs9_{i}", dve.scalar_tensor_tensor(
                        out=bs9[:, :], in0=part[i][:, 0:E], scalar=m9[:, i:i + 1], in1=bs9[:, :],
                        op0=ALU.mult, op1=ALU.add))
                    done(f"ws9_{i}", dve.scalar_tensor_tensor(
                        out=ws9[:, :], in0=part[i][:, E:E + PR], scalar=m9[:, 3 + i:4 + i], in1=ws9[:, :],
                        op0=ALU.mult, op1=ALU.add))
                done("ws9r", dve.tensor_copy(ws9r[:, :, :], ws9[:, :].unsqueeze(1).broadcast_to([P, UR, PR])))

            def z_weights():
                dve.wait_ge(ld_b, 16)
                dve.wait_ge(ld_mx, 16)
                done("gibj", dve.tensor_scalar(gibj[:, :], pb("bj"), pb("gi"), None, ALU.mult))
                done("gjbi", dve.tensor_scalar(gjbi[:, :], pb("gj"), pb("bi"), None, ALU.mult))
                done("gij", dve.tensor_scalar(gij[:, :], pb("gj"), pb("gi"), None, ALU.mult))
                done("mxi", dve.tensor_tensor(mxt[:, :, :], pb("isi").unsqueeze(1).broadcast_to([P, NG, PR]),
                                              gibj[:, :].unsqueeze(2).broadcast_to([P, NG, PR]), ALU.mult))
                done("mxj", dve.tensor_tensor(mx[:, :, 0:PR], pb("isj").rearrange("p (g q) -> p g q", q=PR),
                                              gjbi[:, :].unsqueeze(2).broadcast_to([P, NG, PR]), ALU.mult))
                done("mxs", dve.tensor_tensor(mx[:, :, 0:PR], mx[:, :, 0:PR], mxt[:, :, :], ALU.add))
                done("mxx", dve.tensor_scalar(mx[:, :, 32], pb("isx"), pb("bi"), None, ALU.mult))
                done("mx", dve.tensor_scalar(mx[:, :, 64], pb("bj"), pb("bi"), float(E), ALU.mult, ALU.mult))

            def setup_xt():
                dve.wait_ge(setup_pe, PES["xt"])
                done("xt", dve.tensor_scalar(tt[:, :, 1], po[:, :], pb("gd"), pb("bd"), ALU.mult, ALU.add))

            def top1_bias():
                dve.wait_ge(setup_pe, PES["b1"])
                done("b1e", dve.tensor_tensor(b1e[:, :], po[:, 0:H1 // P], pb("b1"), ALU.add))

            centre_ws()
            expand_weights()
            wsi_sums()
            g_blocks()
            centre_wsi()
            spread_wsi()
            x_stats()
            x_norm()
            split_bias()
            setup_xt()
            z_weights()
            bias_products()
            for i in range(7, 30):
                if 0 <= i - 7 < NU:
                    products(i - 7)
                if 0 <= i - 8 < NU:
                    wt_lo(i - 8)
                if i == 11:
                    top1_bias()
                if (i - 15) % UPT == 0 and 0 <= i - 15 < NU:
                    znt_copy((i - 15) // UPT)
                if 0 <= i - 9 < NU:
                    var_y(i - 9)
                if 0 <= i - 7 < NU:
                    scale_rows(i - 7)
                if 0 <= i - 9 < NU:
                    scale_y(i - 9)
                if (i - 14) % UPT == 0 and 0 <= i - 14 < NU:
                    stats((i - 14) // UPT)
                if (i - 17) % UPT == 0 and 0 <= i - 17 < NU:
                    y_copy((i - 17) // UPT)
                if (i - 14) % UPT == 0 and 0 <= i - 14 < NU:
                    shift_o((i - 14) // UPT)


TABLES = [f"tbl_{f}" for f in range(NF)]


def kernel(**inputs):
    import numpy as _np
    import concourse.bacc as _bacc
    from concourse import mybir as _mybir
    from concourse.bass_utils import run_bass_kernel_spmd as _run

    f = {k: _np.asarray(v) for k, v in inputs.items()}
    tables = [f[n] for n in TABLES]
    offsets = _np.concatenate([[0], _np.cumsum([x.shape[0] for x in tables])[:-1]]).astype(_np.int32)
    row = _np.arange(HALF * NF).reshape(NCH, P).T
    rb, rn = row // NF, row % NF
    lookups = f["ids"].reshape(NT, 2, NCH, P).transpose(3, 0, 2, 1)
    starts = _np.broadcast_to(offsets[rn][:, None, :, None], (P, NT, NCH, 2))

    def rep(v):
        return _np.broadcast_to(v.reshape(1, -1), (P, v.size))

    wsi = f["L0_rec_Wsi"]
    pick = _np.arange(SW)[None, None, :] == (rb - _np.array([b for b, _ in ROWS_OF])[None, :])[:, :, None]
    block = _np.zeros((P, P), _np.float32)
    block[:D, :D] = block[D:, D:] = 1.0 / E
    i_of = _np.arange(P) % PR
    j_of = 4 * _np.arange(NG)[None, :] + _np.arange(P)[:, None] // PR
    gsi, bsi = f["L0_rec_gsi"], f["L0_rec_bsi"]
    one, zero = _np.ones((), gsi.dtype), _np.zeros((), gsi.dtype)
    mask9 = _np.zeros((P, 6), _np.float32)
    for r in range(9):
        mask9[r, r // 3] = mask9[r, 3 + r % 3] = 1.0
    cols = {
        "ident": _np.eye(P), "block": block,
        "wst": _np.concatenate([f["L0_rec_Ws"].T] * 2, 0),
        "wssel": wsi.T[rn].reshape(P, -1), "selmask": pick.reshape(P, -1),
        "eps": _np.full((P, 1), EPS),
        "gsrep": rep(f["L0_rec_gs"]), "one": _np.ones((P, 1)), "wsirep": rep(wsi), "mask9": mask9,
        "gd": f["L0_rec_gd"][:, None], "bd": f["L0_rec_bd"][:, None],
        "gi": gsi[i_of][:, None], "bi": bsi[i_of][:, None],
        "gj": _np.where(j_of == 0, one, gsi[j_of - 1]), "bj": _np.where(j_of == 0, zero, bsi[j_of - 1]),
        "isi": i_of[:, None] == _np.arange(PR), "isj": (j_of[:, :, None] - 1 == _np.arange(PR)).reshape(P, -1),
        "isx": j_of == 0,
        "b1": f["b_top1"].reshape(-1, P).T, "b2": f["b_top2"].reshape(-1, P).T,
        "gl": f["L0_rec_gl"][:USED].reshape(KD, P).T, "bl": f["L0_rec_bl"][:USED].reshape(KD, P).T,
        "w3": f["W_top3"].reshape(-1, P).T,
    }

    def packed(pack):
        out = _np.zeros((P, sum(n for _, n in pack)), _np.float32)
        at = 0
        for name, n in pack:
            out[:, at:at + n] = cols[name]
            at += n
        return out

    tri = (i_of[:, None] + 1) * i_of[:, None] // 2 + j_of
    wl = _np.where((j_of <= i_of[:, None])[:, :, None], f["L0_rec_Wl"].T[_np.where(j_of <= i_of[:, None], tri, 0)], zero)
    w1 = _np.concatenate([f["W_top1"][:USED], f["W_top1"][MAXD:]], 0)
    arrays = {
        "table": _np.concatenate(tables, 0),
        "lookups": lookups, "starts": starts,
        "bsrep": rep(f["L0_rec_bs"]),
        "zxinit": _np.repeat((_np.arange(P) == 64).astype(_np.float32)[:, None], B, 1),
        "zeros": _np.zeros((P, MAXD), _np.float32),
        "pack_a": packed(PACK_A), "pack_b": packed(PACK_B),
        "wdt": f["L0_rec_Wd"].T.reshape(KR, P, E).transpose(1, 0, 2),
        "denset": f["r_dense_t"].T.reshape(KR, P, B).transpose(1, 0, 2),
        "wlt": wl,
        "w1": w1.reshape(KW, P, H1).transpose(1, 0, 2),
        "w2": f["W_top2"].reshape(H1 // P, P, H2).transpose(1, 0, 2),
    }
    arrays = {k: _np.ascontiguousarray(v) for k, v in arrays.items()}
    nc = _bacc.Bacc("TRN2", target_bir_lowering=False, num_devices=1)
    args = {k: nc.dram_tensor(k, v.shape, _mybir.dt.from_np(v.dtype), kind="ExternalInput").ap()
            for k, v in arrays.items()}
    out = nc.dram_tensor("out", (1, B), _mybir.dt.float32, kind="ExternalOutput").ap()
    build(nc, out=out, **args)
    r = _run(nc, [arrays], core_ids=[0])
    return _np.asarray(r.results[0]["out"]).reshape(B, 1)
```

```python
from contextlib import ExitStack

import concourse.bass as bass
from concourse import mybir

F32 = mybir.dt.float32
BF16 = mybir.dt.bfloat16
F16 = mybir.dt.float16
I32 = mybir.dt.int32
ALU = mybir.AluOpType
ACT = mybir.ActivationFunctionType
AX = mybir.AxisListType

P = 128
B = 512
NF = 26
D = 64
E = 128
PR = 32
DD = 256
MAXD = 512
USED = 384
H1 = 512
H2 = 256
EPS = 1e-5

TILE = 128
NT = B // TILE
HALF = TILE // 2
NCH = HALF * NF // P
UR = 16
UPT = HALF // UR
NU = NT * UPT
CHUNKS = [range(0 if m == 0 else (UR * m * NF - 1) // P + 1, (UR * (m + 1) * NF - 1) // P + 1)
          for m in range(UPT)]
ROWS_OF = [(P * c // NF, (P * c + P - 1) // NF) for c in range(NCH)]
SW = 6
YC = 2 + PR
GC = PR + 1
NG = PR // 4
NQ = 4
Z_DVE = 2
FLAT_PARTS = 4
GP = NG // FLAT_PARTS
GSL = 2 * UR // 4
KD = USED // P
KR = DD // P
KW = KD + KR
KH = H1 // P

PACK_A = [("ident", P), ("block", P), ("wst", E), ("wssel", NCH * PR), ("selmask", NCH * SW), ("eps", 1)]
PACK_B = [("gsrep", E), ("one", 1), ("wsirep", PR * NF), ("mask9", 6), ("gd", 1), ("bd", 1),
          ("gi", 1), ("bi", 1), ("gj", NG), ("bj", NG), ("isi", PR), ("isj", NG * PR), ("isx", NG),
          ("b1", H1 // P), ("b2", H2 // P), ("gl", KD), ("bl", KD), ("w3", H2 // P)]


def columns(pack):
    at, out = 0, {}
    for name, n in pack:
        out[name] = (at, at + n)
        at += n
    return out, at


COL_A, NA = columns(PACK_A)
COL_B, NB = columns(PACK_B)


def build(nc, table, lookups, starts, pack_a, pack_b, bsrep, wdt, denset, wlt, w1, w2, out):
    with ExitStack() as ctx:
        def sb(name, shape, dt=F32):
            return ctx.enter_context(nc.sbuf_tensor(name, shape, dt))

        def ps(name, shape):
            return ctx.enter_context(nc.psum_tensor(name, shape, F32))

        def sem(name):
            return ctx.enter_context(nc.semaphore(name))

        a_sb = sb("a_sb", [P, NA])
        b_sb = sb("b_sb", [P, NB])

        def pa(name, rows=slice(0, P)):
            lo, hi = COL_A[name]
            return a_sb[rows, lo:hi]

        def pb(name, rows=slice(0, P)):
            lo, hi = COL_B[name]
            return b_sb[rows, lo:hi]

        rel = sb("rel", [P, NT, NCH, 2], I32)
        first = sb("first", [P, NT, NCH, 2], I32)
        idx = sb("idx", [P, NT * NCH * 2], I32)
        emb = sb("emb", [P, NT * NCH * 2, D])
        prod = sb("prod", [P, 8 * D])
        var = sb("var", [P, NT * NCH * 2])
        std = sb("std", [P, NT * NCH * 2])
        inv = sb("inv", [P, NT * NCH * 2])
        embt = [sb(f"embt{i}", [P, 4 * P]) for i in range(2)]
        wt = [sb(f"wt{i}", [P, 2, UR * PR], F16) for i in range(2)]
        sq = sb("sq", [P, 2, UR * PR])
        vary = [sb(f"vary{i}", [P, 2 * UR]) for i in range(2)]
        stdy = [sb(f"stdy{i}", [P, 2 * UR]) for i in range(2)]
        invy = [sb(f"invy{i}", [P, 2 * UR]) for i in range(2)]
        tt = sb("tt", [P, B, YC])
        zs = [sb(f"zs{i}", [P, NG, TILE]) for i in range(2)]
        zx = sb("zx", [P, B])
        wl = sb("wl", [P, NG, MAXD])
        wx = sb("wx", [P, MAXD])
        mx = sb("mx", [P, NG, 96])
        mxt = sb("mxt", [P, NG, PR])
        w1s = sb("w1s", [P, KW, H1])
        w2s = sb("w2s", [P, H1 // P, H2])
        wds = sb("wds", [P, KR, E])
        dts = sb("dts", [P, KR, B])
        wm = sb("wm", [P, NCH])
        wsel = sb("wsel", [P, NCH, PR])
        sel = sb("sel", [P, NCH, SW, PR])
        mean1 = sb("mean1", [P, 1])
        wsc = sb("wsc", [P, E])
        wsce = sb("wsce", [P, P])
        g2 = sb("g2", [P, P])
        wvf = sb("wvf", [P, E])
        wvh = sb("wvh", [P, E], F16)
        wvl = sb("wvl", [P, E], F16)
        rest = sb("rest", [P, E + PR])
        part = [sb(f"part{i}", [P, E + PR], BF16) for i in range(3)]
        bs9 = sb("bs9", [P, E], BF16)
        ws9 = sb("ws9", [P, PR], BF16)
        ws9r = sb("ws9r", [P, UR, PR], BF16)
        wsum = sb("wsum", [P, PR])
        wmean = sb("wmean", [P, 1])
        xst = sb("xst", [P, NT, 6])
        xmv = sb("xmv", [P, NT, 2])
        xstd = sb("xstd", [P, NT])
        xinv = sb("xinv", [P, NT])
        xnmr = sb("xnmr", [P, NT])
        xn = sb("xn", [P, NT, E])
        gibj = sb("gibj", [P, NG])
        gjbi = sb("gjbi", [P, NG])
        gij = sb("gij", [P, NG])
        ost = sb("ost", [P, 6])
        omv = sb("omv", [P, 2])
        ostd = sb("ostd", [P, 1])
        oinv = sb("oinv", [P, 1])
        zn = sb("zn", [P, USED])
        znt = sb("znt", [P, KD, TILE])
        h1 = sb("h1", [P, H1 // P, TILE])
        h2 = sb("h2", [P, H2 // P, TILE])
        yrow = sb("yrow", [1, B])

        pq = ps("pq", [P, 4 * P])
        pw = [ps(f"pw{i}", [P, 512]) for i in range(2)]
        pv = ps("pv", [P, 2, 512])
        pg = ps("pg", [P, 2, 512])
        po = ps("po", [P, 512])

        ld_rel, ld_first, ld_a, ld_b, ld_x, ld_w1, ld_w2, ld_dt, ld_bs, cleared = (
            sem(n) for n in ("ld_rel", "ld_first", "ld_a", "ld_b", "ld_x", "ld_w1", "ld_w2", "ld_dt",
                              "ld_bs", "cleared"))
        ld_wl = sem("ld_wl")
        idx_ready = sem("idx_ready")
        gathered = [sem(f"gathered{u}") for u in range(NU)]
        setup_v = sem("setup_v")
        setup_pe = sem("setup_pe")
        setup_a = sem("setup_a")
        tr_done, embt_ready, q_done, prod_ready, var_ready, std_ready, inv_ready, scaled = (
            sem(n) for n in ("tr_done", "embt_ready", "q_done", "prod_ready", "var_ready", "std_ready",
                             "inv_ready", "scaled"))
        contracted, hi_ready, wt_ready, v_done, sq_ready, vary_ready, stdy_ready, invy_ready, t_ready = (
            sem(n) for n in ("contracted", "hi_ready", "wt_ready", "v_done", "sq_ready", "vary_ready", "stdy_ready",
                             "invy_ready", "t_ready"))
        gram_done, z_ready, z_late = sem("gram_done"), sem("z_ready"), sem("z_late")
        o_done, ost_ready, omv_ready, ostd_ready, oinv_ready, zn_ready, znt_done, znt_ready = (
            sem(n) for n in ("o_done", "ost_ready", "omv_ready", "ostd_ready", "oinv_ready",
                             "zn_ready", "znt_done", "znt_ready"))
        h1_done, h1_ready, h2_done, h2_ready, y_done, y_ready = (
            sem(n) for n in ("h1_done", "h1_ready", "h2_done", "h2_ready", "y_done", "y_ready"))
        stored = sem("stored")

        def kof(u):
            t, m = divmod(u, UPT)
            return (t * NCH + CHUNKS[m][0]) * 2, 2 * len(CHUNKS[m])

        def o_bank(t):
            return pv[:, 1, :] if t == NT - 1 else po[:, :]

        def h1_sums(t, o):
            if t == NT - 1:
                return (pq[:, 0:P], pw[0][:, 0:P], pw[1][:, 0:P], pv[:, 0, 0:P])[o]
            return po[:, o * P:(o + 1) * P]

        block = ctx.enter_context(nc.Block())

        @block.sync
        def _(sp):
            sp.dma_start(rel[:, :, :, :], lookups).then_inc(ld_rel, 16)
            sp.dma_start(first[:, :, :, :], starts).then_inc(ld_first, 16)
            sp.dma_start(a_sb[:, :], pack_a).then_inc(ld_a, 16)
            sp.dma_start(b_sb[:, :], pack_b).then_inc(ld_b, 16)
            sp.dma_start(rest[:, 0:E], bsrep).then_inc(ld_bs, 16)
            sp.dma_start(wds[:, :, :], wdt).then_inc(ld_x, 16)
            sp.dma_start(dts[:, :, :], denset).then_inc(ld_dt, 16)
            for g in range(NG):
                if g:
                    sp.wait_ge(ld_wl, 16 * g)
                sp.dma_start(wl[:, g, :], wlt[:, g, :]).then_inc(ld_wl, 16)
            sp.wait_ge(ld_wl, 16 * NG)
            for c in range(KW):
                if c:
                    sp.wait_ge(ld_w1, 16 * c)
                sp.dma_start(w1s[:, c, :], w1[:, c, :]).then_inc(ld_w1, 16)
            sp.wait_ge(ld_w1, 16 * KW)
            sp.dma_start(w2s[:, :, :], w2).then_inc(ld_w2, 16)
            sp.wait_ge(y_ready, NT)
            sp.dma_start(out, yrow[:, :]).then_inc(stored, 16)
            sp.wait_ge(stored, 16)

        @block.gpsimd
        def _(pool):
            pool.memset(zx[:, :], 0.0).then_inc(cleared, 1)
            pool.wait_ge(cleared, 1)
            pool.memset(zx[64:65, :], 1.0).then_inc(cleared, 1)
            pool.wait_ge(cleared, 2)
            pool.memset(wx[96:P, :], 0.0).then_inc(cleared, 1)
            pool.wait_ge(cleared, 3)
            pool.memset(mx[:, :, PR:], 0.0).then_inc(cleared, 1)
            pool.wait_ge(cleared, 4)
            pool.wait_ge(ld_rel, 16)
            pool.wait_ge(ld_first, 16)
            pool.tensor_tensor(idx[:, :], rel[:, :, :, :].rearrange("p t c s -> p (t c s)"),
                               first[:, :, :, :].rearrange("p t c s -> p (t c s)"), ALU.add).then_inc(idx_ready, 1)
            pool.wait_ge(idx_ready, 1)
            for u in range(NU):
                k0, nk = kof(u)
                for k in range(k0, k0 + nk):
                    pool.indirect_dma_start(emb[:, k, :], None, table,
                                            bass.IndirectOffsetOnAxis(ap=idx[:, k:k + 1], axis=0)
                                            ).then_inc(gathered[u], 16)

        def numbered(*names):
            return {n: i + 1 for i, n in enumerate(names)}

        V = numbered(
            "wsum1", "wmean1", "wsc", "selsum", "selmean", "selc", "g2", "wvf", "wvh",
            "wvl", "wsum", "wsumsum", "wmean", "rest0", "gibj", "gjbi", "gij", "mxi",
            "mxj", "mxs", "mxx", "mx", "xst", "xmv", "xinv", "xnmr", "sel0", "part0",
            "left0", "part1", "left1", "part2", "sel", "bs9_0", "ws9_0", "bs9_1", "ws9_1",
            "bs9_2", "ws9_2", "ws9r")
        PES = numbered(
            "wsct", "g", "x", "xt", "xs", "wx")
        AS = numbered(
            "table", "wsce", "xstd", "xn", "ones", "xt", "xs", "wls0", "wls1", "wls2",
            "wls3", "wx")
        @block.tensor
        def _(pe):
            def transposes(u):
                k0, nk = kof(u)
                pe.wait_ge(gathered[u], 16 * nk)
                if u:
                    pe.wait_ge(prod_ready, u)
                else:
                    pe.wait_ge(ld_a, 16)
                for c in range(nk // 2):
                    mm = pe.transpose(pq[:, c * P:(c + 1) * P],
                                      emb[:, k0 + 2 * c:k0 + 2 * c + 2, :].rearrange("p s d -> p (s d)"), pa("ident"))
                mm.then_inc(tr_done, 1)

            def quadratic(u):
                pe.wait_ge(embt_ready, u + 1)
                _, nk = kof(u)
                for c in range(nk // 2):
                    mm = pe.matmul(pq[:, c * P:(c + 1) * P], embt[u % 2][:, c * P:(c + 1) * P], g2[:, :],
                                   start=True, stop=True)
                mm.then_inc(q_done, 1)

            def contract(u):
                t, m = divmod(u, UPT)
                pe.wait_ge(scaled, u + 1)
                if u < 2:
                    pe.wait_ge(setup_v, V["sel" if u else "sel0"])
                if u:
                    pe.wait_ge(wt_ready, 2 * u)
                for c in CHUNKS[m]:
                    b0, b1 = ROWS_OF[c]
                    k = (t * NCH + c) * 2
                    lhs = emb[:, k:k + 2, :].rearrange("p s d -> p (s d)")
                    for mm_ in (m, m + 1):
                        lo, hi = max(b0, UR * mm_), min(b1 + 1, UR * (mm_ + 1))
                        if lo >= hi:
                            continue
                        mm = pe.matmul(pw[(t * UPT + mm_) % 2][:, (lo - UR * mm_) * PR:(hi - UR * mm_) * PR],
                                       lhs, sel[:, c, lo - b0:hi - b0, :].rearrange("p j q -> p (j q)"),
                                       start=(mm_ > m or (m == 0 and c == 0)), stop=True, skip_group_check=True)
                mm.then_inc(contracted, 1)

            def expand(u, s):
                pe.wait_ge(wt_ready, 2 * u + s + 1)
                if u == 0 and s == 0:
                    pe.wait_ge(setup_v, V["ws9r"])
                if u:
                    pe.wait_ge(t_ready, 2 * u - 1 + s)
                pe.matmul(pv[:, s, :], wvh[:, :], wt[u % 2][:, s, :], start=True, stop=False)
                pe.matmul(pv[:, s, :], wvl[:, :], wt[u % 2][:, s, :], start=False, stop=False)
                pe.matmul(pv[:, s, :], bs9[:, :], ws9r[:, :, :].rearrange("p b q -> p (b q)"),
                          start=False, stop=True).then_inc(v_done, 1)

            def gram(u):
                t, m = divmod(u, UPT)
                pe.wait_ge(t_ready, 2 * u + 2)
                if u == 0:
                    pe.wait_ge(setup_a, AS["xt"])
                    pe.wait_ge(setup_a, AS["ones"])
                if u >= 2 and u % 2 == 0:
                    pe.wait_ge(z_ready, NQ * (u // 2))
                for s in range(2):
                    for j in range(UR):
                        b = t * TILE + s * HALF + UR * m + j
                        q, slot = j % 4, (m % 2) * 4 + j // 4
                        mm = pe.matmul(pg[32 * q:32 * q + 32, s, slot * GC:(slot + 1) * GC],
                                       tt[:, b, 2:YC], tt[:, b, 0:GC], start=True, stop=True)
                mm.then_inc(gram_done, 1)

            def flat_linear(t, part):
                if part == 0:
                    if t < NT - 1:
                        pe.wait_ge(z_ready, NQ * (2 * t + 2))
                    else:
                        pe.wait_ge(z_ready, NQ * (2 * t + 2) - Z_DVE)
                        pe.wait_ge(z_late, Z_DVE)
                    if t == NT - 1:
                        pe.wait_ge(t_ready, 2 * NU)
                    elif t:
                        pe.wait_ge(y_ready, t)
                    else:
                        pe.wait_ge(setup_a, AS["wx"])
                        pe.wait_ge(setup_a, AS["wls3"])
                for g in range(GP * part, GP * part + GP):
                    pe.matmul(o_bank(t), zs[t % 2][:, g, :], wl[:, g, :], start=(g == 0), stop=False)
                if part == FLAT_PARTS - 1:
                    pe.matmul(o_bank(t), zx[:, t * TILE:(t + 1) * TILE], wx[:, :], start=False, stop=True
                              ).then_inc(o_done, 1)

            def z_transposes(t):
                pe.wait_ge(zn_ready, t + 1)
                for c in range(KD):
                    mm = pe.transpose(o_bank(t)[:, c * P:(c + 1) * P], zn[:, c * P:(c + 1) * P], pa("ident"))
                mm.then_inc(znt_done, 1)

            def top1_dense(t):
                if t == NT - 1:
                    pe.wait_ge(prod_ready, NU)
                    pe.wait_ge(wt_ready, 2 * NU)
                    pe.wait_ge(t_ready, 2 * NU)
                else:
                    pe.wait_ge(znt_ready, t + 1)
                if t == 0:
                    pe.wait_ge(ld_w1, 16 * KW)
                for o in range(H1 // P):
                    for c in range(KD, KW):
                        pe.matmul(h1_sums(t, o), w1s[:, c, o * P:(o + 1) * P],
                                  dts[:, c - KD, t * TILE:(t + 1) * TILE], start=(c == KD and (o == 0 or t == NT - 1)), stop=False,
                                  skip_group_check=True)

            def top1(t, o):
                if o == 0:
                    pe.wait_ge(znt_ready, t + 1)
                for c in range(KD):
                    mm = pe.matmul(h1_sums(t, o), w1s[:, c, o * P:(o + 1) * P], znt[:, c, :],
                                   start=False, stop=(c == KD - 1), skip_group_check=True)
                mm.then_inc(h1_done, 1)

            def top2(t, c):
                pe.wait_ge(h1_ready, KH * t + (c + 1 if t == NT - 1 else KH))
                if t == 0 and c == 0:
                    pe.wait_ge(ld_w2, 16)
                if t == NT - 1 and c == 0:
                    pe.wait_ge(y_ready, t)
                for o in range(H2 // P):
                    mm = pe.matmul(po[:, o * P:(o + 1) * P], w2s[:, c, o * P:(o + 1) * P], h1[:, c, :],
                                   start=(c == 0 and o == 0), stop=(c == KH - 1), skip_group_check=True)
                if c == KH - 1:
                    mm.then_inc(h2_done, 1)

            def top3(t):
                pe.wait_ge(h2_ready, t + 1)
                for c in range(H2 // P):
                    mm = pe.matmul(po[0:1, 0:P], pb("w3")[:, c:c + 1], h2[:, c, :],
                                   start=(c == 0), stop=(c == H2 // P - 1))
                mm.then_inc(y_done, 1)

            def transpose_ws():
                pe.wait_ge(ld_a, 16)
                pe.wait_ge(setup_v, V["wsc"])
                pe.transpose(po[:, 0:P], wsc[:, :], pa("ident")).then_inc(setup_pe, 1)

            def g_product():
                pe.wait_ge(setup_a, AS["wsce"])
                pe.matmul(po[:, 0:P], wsce[:, :], wsce[:, :], start=True, stop=True).then_inc(setup_pe, 1)

            def x_product():
                pe.wait_ge(setup_v, V["g2"])
                pe.wait_ge(ld_x, 16)
                pe.wait_ge(ld_dt, 16)
                for t in range(NT):
                    for c in range(KR):
                        mm = pe.matmul(po[:, t * E:(t + 1) * E], dts[:, c, t * TILE:(t + 1) * TILE], wds[:, c, :],
                                       start=(c == 0), stop=(c == KR - 1))
                mm.then_inc(setup_pe, 1)

            def x_transposes():
                pe.wait_ge(setup_a, AS["xn"])
                for t in range(NT):
                    mm = pe.transpose(po[:, t * TILE:(t + 1) * TILE], xn[:, t, :], pa("ident"))
                mm.then_inc(setup_pe, 1)

            def x_sums():
                pe.wait_ge(setup_a, AS["xt"])
                pe.wait_ge(setup_a, AS["ones"])
                pe.matmul(po[32:33, 0:B], tt[:, 0, 0:1], tt[:, :, 1], start=True, stop=True).then_inc(setup_pe, 1)

            def zx_weights(part):
                if part == 0:
                    pe.wait_ge(setup_a, AS["xs"])
                    pe.wait_ge(setup_v, V["mx"])
                    pe.wait_ge(ld_wl, 16 * NG)
                for g in range(GP * part, GP * part + GP):
                    mm = pe.matmul(po[0:96, :], mx[:, g, :], wl[:, g, :], start=(g == 0), stop=(g == NG - 1))
                if part == FLAT_PARTS - 1:
                    mm.then_inc(setup_pe, 1)

            transpose_ws()
            g_product()
            x_product()
            x_transposes()
            for i in range(21):
                if (i - 12) % UPT == 0 and 0 <= i - 12 < NU - UPT:
                    top2((i - 12) // UPT, 1)
                if (i - 10) % UPT == 0 and 0 <= i - 10 < NU - UPT:
                    top1_dense((i - 10) // UPT)
                if (i - 12) % UPT == 0 and 0 <= i - 12 < NU - UPT:
                    top2((i - 12) // UPT, 2)
                if i == 4:
                    zx_weights(2)
                if (i - 12) % UPT == 0 and 0 <= i - 12 < NU - UPT:
                    top2((i - 12) // UPT, 3)
                if i == 1:
                    x_sums()
                if 0 <= i - 3 < NU:
                    expand(i - 3, 0)
                    expand(i - 3, 1)
                if i == 20:
                    flat_linear(NT - 1, 0)
                if (i - 12) % UPT == 0 and 0 <= i - 12 < NU - UPT:
                    top3((i - 12) // UPT)
                if (i - 10) % UPT == 0 and 0 <= i - 10 < NU - UPT:
                    top1((i - 10) // UPT, 0)
                if 0 <= i - 2 < NU:
                    contract(i - 2)
                if i == 3:
                    zx_weights(0)
                if i == 4:
                    zx_weights(3)
                if (i - 8) % UPT == 0 and 0 <= i - 8 < NU - UPT:
                    flat_linear((i - 8) // UPT, 0)
                if (i - 9) % UPT == 0 and 0 <= i - 9 < NU - UPT:
                    z_transposes((i - 9) // UPT)
                if (i - 8) % UPT == 0 and 0 <= i - 8 < NU - UPT:
                    flat_linear((i - 8) // UPT, 1)
                if (i - 10) % UPT == 0 and 0 <= i - 10 < NU - UPT:
                    top1((i - 10) // UPT, 1)
                if 0 <= i < NU:
                    transposes(i)
                if (i - 8) % UPT == 0 and 0 <= i - 8 < NU - UPT:
                    flat_linear((i - 8) // UPT, 2)
                if (i - 10) % UPT == 0 and 0 <= i - 10 < NU - UPT:
                    top1((i - 10) // UPT, 2)
                if (i - 8) % UPT == 0 and 0 <= i - 8 < NU - UPT:
                    flat_linear((i - 8) // UPT, 3)
                if (i - 10) % UPT == 0 and 0 <= i - 10 < NU - UPT:
                    top1((i - 10) // UPT, 3)
                if 0 <= i - 4 < NU:
                    gram(i - 4)
                if i == 3:
                    zx_weights(1)
                if (i - 11) % UPT == 0 and 0 <= i - 11 < NU - UPT:
                    top2((i - 11) // UPT, 0)
                if 0 <= i < NU:
                    quadratic(i)
            flat_linear(NT - 1, 1)
            flat_linear(NT - 1, 2)
            flat_linear(NT - 1, 3)
            top1_dense(NT - 1)
            z_transposes(NT - 1)
            top1(NT - 1, 0)
            top1(NT - 1, 1)
            top1(NT - 1, 2)
            top1(NT - 1, 3)
            top2(NT - 1, 0)
            top2(NT - 1, 1)
            top2(NT - 1, 2)
            top2(NT - 1, 3)
            top3(NT - 1)

        def z_parts(h, q):
            t = h // 2
            b0 = 32 * (h % 2) + q
            src = pg[32 * q:32 * q + 32, :, 0:GSL * GC].rearrange("p s (l c) -> p s l c", c=GC)
            dst = zs[t % 2][:, :, :].rearrange("p g (s r) -> p s r g", s=2)
            return [(src[:, :, :, 1 + j:GC:4], dst[32 * j:32 * j + 32, :, b0:b0 + 29:4, :]) for j in range(4)]

        def zx_part(h, q):
            t = h // 2
            b0 = 32 * (h % 2) + q
            src = pg[32 * q:32 * q + 32, :, 0:GSL * GC].rearrange("p s (l c) -> p s l c", c=GC)[:, :, :, 0]
            dst = zx[0:32, t * TILE:(t + 1) * TILE].rearrange("p (s r) -> p s r", s=2)[:, :, b0:b0 + 29:4]
            return src, dst

        @block.scalar
        def _(act):
            def embt_copy(u):
                act.wait_ge(tr_done, u + 1)
                if u >= 2:
                    act.wait_ge(q_done, u - 1)
                _, nk = kof(u)
                n = nk // 2 * P
                act.activation(embt[u % 2][:, 0:n], pq[:, 0:n], ACT.Copy).then_inc(embt_ready, 1)

            def std_rows(u):
                k0, nk = kof(u)
                act.wait_ge(var_ready, u + 1)
                act.activation(std[:, k0:k0 + nk], var[:, k0:k0 + nk], ACT.Sqrt, bias=pa("eps")).then_inc(std_ready, 1)

            def wt_hi(u, s):
                act.wait_ge(contracted, u + 1)
                if u >= 2:
                    act.wait_ge(v_done, 2 * u - 2)
                here = slice(D * s, D * s + D)
                act.activation(wt[u % 2][here, s, :], pw[u % 2][here, :], ACT.Copy).then_inc(hi_ready, 1)

            def squares(u, s):
                act.wait_ge(v_done, 2 * u + s + 1)
                if u:
                    act.wait_ge(vary_ready, 2 * u - 1 + s)
                act.activation(sq[:, s, :], pv[:, s, :], ACT.Square, scale=float(PR) ** -0.5).then_inc(sq_ready, 1)

            def std_y(u):
                act.wait_ge(vary_ready, 2 * u + 2)
                if u >= 2:
                    act.wait_ge(invy_ready, u - 1)
                act.activation(stdy[u % 2][:, :], vary[u % 2][:, :], ACT.Sqrt, bias=pa("eps")).then_inc(stdy_ready, 1)

            def z_copies(h, q):
                act.wait_ge(gram_done, 2 * h + 2)
                if h % 2 == 0 and h >= 4:
                    act.wait_ge(o_done, h // 2 - 1)
                for src, dst in z_parts(h, q):
                    act.activation(dst, src, ACT.Copy)
                src, dst = zx_part(h, q)
                act.activation(dst, src, ACT.Copy).then_inc(z_ready, 1)

            def std_o(t):
                act.wait_ge(omv_ready, t + 1)
                act.activation(ostd[:, :], omv[:, 1:2], ACT.Sqrt, bias=pa("eps")).then_inc(ostd_ready, 1)

            def relu1(t, o):
                if t == NT - 1 and o == 0:
                    act.wait_ge(h2_done, t)
                act.wait_ge(h1_done, KH * t + (o + 1 if t == NT - 1 else KH))
                act.activation(h1[:, o, :], h1_sums(t, o), ACT.Relu, bias=pb("b1")[:, o:o + 1]
                               ).then_inc(h1_ready, 1)

            def relu2(t):
                act.wait_ge(h2_done, t + 1)
                for o in range(H2 // P):
                    last = act.activation(h2[:, o, :], po[:, o * P:(o + 1) * P], ACT.Relu,
                                          bias=pb("b2")[:, o:o + 1])
                last.then_inc(h2_ready, 1)

            def load_table():
                act.wait_ge(ld_a, 16)
                act.activation(ostd[:, :], pa("eps"), ACT.Sqrt).then_inc(setup_a, 1)

            def wsce_copy():
                act.wait_ge(setup_pe, PES["wsct"])
                act.activation(wsce[:, :], po[:, 0:P], ACT.Copy).then_inc(setup_a, 1)

            def ones():
                act.wait_ge(ld_b, 16)
                act.activation(tt[:, :, 0], pb("one").broadcast_to([P, B]), ACT.Copy).then_inc(setup_a, 1)

            def std_x():
                act.wait_ge(setup_v, V["xmv"])
                act.activation(xstd[:, :], xmv[:, :, 1], ACT.Sqrt, bias=pa("eps")).then_inc(setup_a, 1)

            def x_norm():
                act.wait_ge(setup_v, V["xnmr"])
                for t in range(NT):
                    last = act.activation(xn[:, t, :], po[:, t * E:(t + 1) * E], ACT.Identity,
                                          bias=xnmr[:, t:t + 1], scale=xinv[:, t:t + 1])
                last.then_inc(setup_a, 1)

            def x_affine():
                act.wait_ge(setup_pe, PES["xt"])
                act.activation(tt[:, :, 1], po[:, :], ACT.Identity, bias=pb("bd"), scale=pb("gd")).then_inc(setup_a, 1)

            def x_sums_copy():
                act.wait_ge(setup_pe, PES["xs"])
                act.wait_ge(cleared, 4)
                act.activation(zx[32:33, :], po[32:33, 0:B], ACT.Copy).then_inc(setup_a, 1)

            def zx_weights_copy():
                act.wait_ge(setup_pe, PES["wx"])
                act.activation(wx[0:96, :], po[0:96, :], ACT.Copy).then_inc(setup_a, 1)

            def scale_wl(part):
                act.wait_ge(setup_pe, PES["wx"])
                act.wait_ge(setup_v, V["gij"])
                for g in range(GP * part, GP * part + GP):
                    last = act.activation(wl[:, g, :], wl[:, g, :], ACT.Copy, scale=gij[:, g:g + 1])
                last.then_inc(setup_a, 1)

            load_table()
            wsce_copy()
            std_x()
            x_norm()
            ones()
            x_affine()
            for i in range(4, 24):
                if 0 <= i - 7 < NU:
                    squares(i - 7, 1)
                if 0 <= i - 5 < NU:
                    std_rows(i - 5)
                if (i - 15) % UPT == 0 and 0 <= i - 15 < NU - UPT:
                    relu1((i - 15) // UPT, 3)
                if 0 <= i - 6 < NU:
                    wt_hi(i - 6, 0)
                if i == 11:
                    zx_weights_copy()
                if 0 <= i - 7 < NU:
                    std_y(i - 7)
                if 0 <= i - 4 < NU:
                    embt_copy(i - 4)
                if 0 <= i - 6 < NU:
                    wt_hi(i - 6, 1)
                if i == 10:
                    scale_wl(2)
                if i == 8:
                    scale_wl(0)
                    scale_wl(1)
                if (i - 14) % UPT == 0 and 0 <= i - 14 < NU - UPT:
                    relu1((i - 14) // UPT, 0)
                    relu1((i - 14) // UPT, 1)
                if (i - 9) % 2 == 0 and 0 <= i - 9 < NU:
                    z_copies((i - 9) // 2, 0)
                    z_copies((i - 9) // 2, 1)
                if (i - 9) % 2 == 0 and 0 <= i - 9 < NU - 2:
                    z_copies((i - 9) // 2, 2)
                if (i - 15) % UPT == 0 and 0 <= i - 15 < NU - UPT:
                    relu2((i - 15) // UPT)
                if i == 10:
                    scale_wl(3)
                if (i - 14) % UPT == 0 and 0 <= i - 14 < NU - UPT:
                    relu1((i - 14) // UPT, 2)
                if (i - 12) % UPT == 0 and 0 <= i - 12 < NU - UPT:
                    std_o((i - 12) // UPT)
                if i == 6:
                    x_sums_copy()
                if (i - 9) % 2 == 0 and 0 <= i - 9 < NU - 2:
                    z_copies((i - 9) // 2, 3)
                if 0 <= i - 6 < NU:
                    squares(i - 6, 0)
            std_o(NT - 1)
            relu1(NT - 1, 0)
            relu1(NT - 1, 1)
            relu1(NT - 1, 2)
            relu1(NT - 1, 3)
            relu2(NT - 1)

        @block.vector
        def _(dve):
            def products(u):
                k0, nk = kof(u)
                dve.wait_ge(q_done, u + 1)
                if u:
                    dve.wait_ge(var_ready, u)
                dve.tensor_tensor(prod[:, 0:nk * D], pq[:, 0:nk * D],
                                  emb[:, k0:k0 + nk, :].rearrange("p k d -> p (k d)"), ALU.mult
                                  ).then_inc(prod_ready, 1)
                dve.wait_ge(prod_ready, u + 1)
                dve.tensor_reduce(var[:, k0:k0 + nk], prod[:, 0:nk * D].rearrange("p (k d) -> p k d", d=D),
                                  AX.X, ALU.add).then_inc(var_ready, 1)

            def scale_rows(u):
                k0, nk = kof(u)
                dve.wait_ge(std_ready, u + 1)
                dve.reciprocal(inv[:, k0:k0 + nk], std[:, k0:k0 + nk]).then_inc(inv_ready, 1)
                dve.wait_ge(inv_ready, u + 1)
                dve.tensor_tensor(emb[:, k0:k0 + nk, :], emb[:, k0:k0 + nk, :],
                                  inv[:, k0:k0 + nk].unsqueeze(2).broadcast_to([P, nk, D]), ALU.mult
                                  ).then_inc(scaled, 1)

            def wt_lo(u, s):
                dve.wait_ge(hi_ready, 2 * u + s + 1)
                here, other = slice(D * s, D * s + D), slice(D * (1 - s), D * (1 - s) + D)
                dve.tensor_tensor(wt[u % 2][other, s, :], pw[u % 2][here, :], wt[u % 2][here, s, :],
                                  ALU.subtract).then_inc(wt_ready, 1)

            def var_y(u, s):
                dve.wait_ge(sq_ready, 2 * u + s + 1)
                if u >= 2:
                    dve.wait_ge(stdy_ready, u - 1)
                dve.tensor_reduce(vary[u % 2][:, s * UR:(s + 1) * UR], sq[:, s, :].rearrange("p (b q) -> p b q", q=PR),
                                  AX.X, ALU.add).then_inc(vary_ready, 1)

            def scale_y(u, s):
                t, m = divmod(u, UPT)
                if s == 0:
                    dve.wait_ge(stdy_ready, u + 1)
                    dve.reciprocal(invy[u % 2][:, :], stdy[u % 2][:, :]).then_inc(invy_ready, 1)
                    dve.wait_ge(invy_ready, u + 1)
                b = t * TILE + s * HALF + UR * m
                dve.tensor_tensor(
                    tt[:, b:b + UR, 2:YC], pv[:, s, :].rearrange("p (b q) -> p b q", q=PR),
                    invy[u % 2][:, s * UR:(s + 1) * UR].unsqueeze(2).broadcast_to([P, UR, PR]), ALU.mult
                    ).then_inc(t_ready, 1)

            def z_copies(h, q):
                dve.wait_ge(gram_done, 2 * h + 2)
                for src, dst in z_parts(h, q):
                    dve.tensor_copy(dst, src)
                src, dst = zx_part(h, q)
                dve.tensor_copy(dst, src).then_inc(z_late, 1)

            def stats(t):
                dve.wait_ge(o_done, t + 1)
                dve.bn_stats(ost[:, :], o_bank(t)).then_inc(ost_ready, 1)
                dve.wait_ge(ost_ready, t + 1)
                dve.bn_aggr(omv[:, :], ost[:, :]).then_inc(omv_ready, 1)

            def normalise(t):
                dve.wait_ge(ostd_ready, t + 1)
                dve.reciprocal(oinv[:, :], ostd[:, :]).then_inc(oinv_ready, 1)
                dve.wait_ge(oinv_ready, t + 1)
                dve.tensor_scalar(zn[:, :], o_bank(t)[:, 0:USED], omv[:, 0:1], oinv[:, :], ALU.subtract, ALU.mult
                                  ).then_inc(zn_ready, 1)

            def znt_scale(t):
                dve.wait_ge(znt_done, t + 1)
                if t:
                    dve.wait_ge(h1_done, KH * t)
                for c in range(KD):
                    last = dve.tensor_scalar(znt[:, c, :], o_bank(t)[:, c * P:(c + 1) * P], pb("gl")[:, c:c + 1],
                                             pb("bl")[:, c:c + 1], ALU.mult, ALU.add)
                last.then_inc(znt_ready, 1)

            def y_copy(t):
                dve.wait_ge(y_done, t + 1)
                dve.tensor_copy(yrow[:, t * TILE:(t + 1) * TILE], po[0:1, 0:P]).then_inc(y_ready, 1)

            def done(name, ins, needed=True):
                ins.then_inc(setup_v, 1)
                if needed:
                    dve.wait_ge(setup_v, V[name])

            def centre_ws():
                dve.wait_ge(ld_a, 16)
                done("wsum1", dve.tensor_reduce(mean1[:, :], pa("wst"), AX.X, ALU.add))
                done("wmean1", dve.tensor_scalar(mean1[:, :], mean1[:, :], 1.0 / E, None, ALU.mult))
                done("wsc", dve.tensor_scalar(wsc[:, :], pa("wst"), mean1[:, :], None, ALU.subtract))

            def centre_wsi():
                wssel = pa("wssel").rearrange("p (c q) -> p c q", q=PR)
                done("selsum", dve.tensor_reduce(wm[:, :], wssel, AX.X, ALU.add))
                done("selmean", dve.tensor_scalar(wm[:, :], wm[:, :], 1.0 / PR, None, ALU.mult))
                done("selc", dve.tensor_tensor(wsel[:, :, :], wssel,
                                               wm[:, :].unsqueeze(2).broadcast_to([P, NCH, PR]), ALU.subtract))

            def spread_wsi():
                done("sel0", spread(CHUNKS[0]))

            def spread(chunks):
                c = slice(chunks[0], chunks[-1] + 1)
                return dve.tensor_tensor(
                    sel[:, c, :, :], wsel[:, c, :].unsqueeze(2).broadcast_to([P, len(chunks), SW, PR]),
                    pa("selmask").rearrange("p (c j) -> p c j", j=SW)[:, c, :].unsqueeze(3)
                    .broadcast_to([P, len(chunks), SW, PR]), ALU.mult)

            def spread_wsi_rest():
                done("sel", spread(range(CHUNKS[1][0], NCH)))

            def g_blocks():
                dve.wait_ge(setup_pe, PES["g"])
                done("g2", dve.tensor_tensor(g2[:, :], po[:, 0:P], pa("block"), ALU.mult))

            def x_stats():
                dve.wait_ge(setup_pe, PES["x"])
                for t in range(NT):
                    last = dve.bn_stats(xst[:, t, :], po[:, t * E:(t + 1) * E])
                done("xst", last)
                for t in range(NT):
                    last = dve.bn_aggr(xmv[:, t, :], xst[:, t, :])
                done("xmv", last)

            def x_factors():
                dve.wait_ge(setup_a, AS["xstd"])
                done("xinv", dve.reciprocal(xinv[:, :], xstd[:, :]))
                done("xnmr", dve.scalar_tensor_tensor(out=xnmr[:, :], in0=xmv[:, :, 0], scalar=-1.0, in1=xinv[:, :],
                                                      op0=ALU.mult, op1=ALU.mult))

            def expand_weights():
                dve.wait_ge(ld_b, 16)
                done("wvf", dve.tensor_tensor(wvf[:, :], wsc[:, :], pb("gsrep"), ALU.mult))
                done("wvh", dve.tensor_copy(wvh[:, :], wvf[:, :]))
                done("wvl", dve.tensor_tensor(wvl[:, :], wvf[:, :], wvh[:, :], ALU.subtract))

            def wsi_sums():
                dve.wait_ge(ld_b, 16)
                done("wsum", dve.tensor_reduce(wsum[:, :], pb("wsirep").rearrange("p (q n) -> p q n", n=NF),
                                               AX.X, ALU.add))
                done("wsumsum", dve.tensor_reduce(wmean[:, :], wsum[:, :], AX.X, ALU.add))
                done("wmean", dve.tensor_scalar(wmean[:, :], wmean[:, :], 1.0 / PR, None, ALU.mult))
                done("rest0", dve.tensor_scalar(rest[:, E:E + PR], wsum[:, :], wmean[:, :], None, ALU.subtract))

            def split_bias():
                dve.wait_ge(ld_bs, 16)
                for i in range(3):
                    done(f"part{i}", dve.tensor_copy(part[i][:, :], rest[:, :]))
                    if i < 2:
                        done(f"left{i}", dve.tensor_tensor(rest[:, :], rest[:, :], part[i][:, :], ALU.subtract))

            def bias_products():
                m9 = pb("mask9")
                done("bs9_0", needed=False, ins=dve.tensor_scalar(bs9[:, :], part[0][:, 0:E], m9[:, 0:1], None, ALU.mult))
                done("ws9_0", dve.tensor_scalar(ws9[:, :], part[0][:, E:E + PR], m9[:, 3:4], None, ALU.mult))
                for i in (1, 2):
                    done(f"bs9_{i}", needed=False, ins=dve.scalar_tensor_tensor(
                        out=bs9[:, :], in0=part[i][:, 0:E], scalar=m9[:, i:i + 1], in1=bs9[:, :],
                        op0=ALU.mult, op1=ALU.add))
                    done(f"ws9_{i}", dve.scalar_tensor_tensor(
                        out=ws9[:, :], in0=part[i][:, E:E + PR], scalar=m9[:, 3 + i:4 + i], in1=ws9[:, :],
                        op0=ALU.mult, op1=ALU.add))
                done("ws9r", dve.tensor_copy(ws9r[:, :, :], ws9[:, :].unsqueeze(1).broadcast_to([P, UR, PR])))

            def z_weights():
                dve.wait_ge(ld_b, 16)
                dve.wait_ge(cleared, 4)
                done("gibj", needed=False, ins=dve.tensor_scalar(gibj[:, :], pb("bj"), pb("gi"), None, ALU.mult))
                done("gjbi", needed=False, ins=dve.tensor_scalar(gjbi[:, :], pb("gj"), pb("bi"), None, ALU.mult))
                done("gij", dve.tensor_scalar(gij[:, :], pb("gj"), pb("gi"), None, ALU.mult))
                done("mxi", needed=False, ins=dve.tensor_tensor(mxt[:, :, :], pb("isi").unsqueeze(1).broadcast_to([P, NG, PR]),
                                              gibj[:, :].unsqueeze(2).broadcast_to([P, NG, PR]), ALU.mult))
                done("mxj", dve.tensor_tensor(mx[:, :, 0:PR], pb("isj").rearrange("p (g q) -> p g q", q=PR),
                                              gjbi[:, :].unsqueeze(2).broadcast_to([P, NG, PR]), ALU.mult))
                done("mxs", dve.tensor_tensor(mx[:, :, 0:PR], mx[:, :, 0:PR], mxt[:, :, :], ALU.add))
                done("mxx", needed=False, ins=dve.tensor_scalar(mx[:, :, 32], pb("isx"), pb("bi"), None, ALU.mult))
                done("mx", dve.tensor_scalar(mx[:, :, 64], pb("bj"), pb("bi"), float(E), ALU.mult, ALU.mult))

            centre_ws()
            centre_wsi()
            g_blocks()
            expand_weights()
            wsi_sums()
            z_weights()
            x_stats()
            x_factors()
            spread_wsi()
            split_bias()
            spread_wsi_rest()
            bias_products()
            for i in range(4, 23):
                if (i - 12) % UPT == 0 and 0 <= i - 12 < NU - UPT:
                    normalise((i - 12) // UPT)
                if 0 <= i - 4 < NU:
                    products(i - 4)
                if 0 <= i - 6 < NU:
                    var_y(i - 6, 0)
                    var_y(i - 6, 1)
                if (i - 12) % UPT == 0 and 0 <= i - 12 < NU - UPT:
                    znt_scale((i - 12) // UPT)
                if 0 <= i - 5 < NU:
                    wt_lo(i - 5, 0)
                if 0 <= i - 6 < NU:
                    scale_y(i - 6, 0)
                if i == 22:
                    z_copies(2 * NT - 1, 2)
                if 0 <= i - 5 < NU:
                    wt_lo(i - 5, 1)
                if 0 <= i - 6 < NU:
                    scale_y(i - 6, 1)
                if i == 22:
                    z_copies(2 * NT - 1, 3)
                if 0 <= i - 4 < NU:
                    scale_rows(i - 4)
                if (i - 14) % UPT == 0 and 0 <= i - 14 < NU - UPT:
                    y_copy((i - 14) // UPT)
                if (i - 11) % UPT == 0 and 0 <= i - 11 < NU - UPT:
                    stats((i - 11) // UPT)
            stats(NT - 1)
            normalise(NT - 1)
            znt_scale(NT - 1)
            y_copy(NT - 1)


TABLES = [f"tbl_{f}" for f in range(NF)]


def kernel(**inputs):
    import numpy as _np
    import concourse.bacc as _bacc
    from concourse import mybir as _mybir
    from concourse.bass_utils import run_bass_kernel_spmd as _run

    f = {k: _np.asarray(v) for k, v in inputs.items()}
    tables = [f[n] for n in TABLES]
    offsets = _np.concatenate([[0], _np.cumsum([x.shape[0] for x in tables])[:-1]]).astype(_np.int32)
    row = _np.arange(HALF * NF).reshape(NCH, P).T
    rb, rn = row // NF, row % NF
    lookups = f["ids"].reshape(NT, 2, NCH, P).transpose(3, 0, 2, 1)
    starts = _np.broadcast_to(offsets[rn][:, None, :, None], (P, NT, NCH, 2))

    def rep(v):
        return _np.broadcast_to(v.reshape(1, -1), (P, v.size))

    wsi = f["L0_rec_Wsi"]
    pick = _np.arange(SW)[None, None, :] == (rb - _np.array([b for b, _ in ROWS_OF])[None, :])[:, :, None]
    block = _np.zeros((P, P), _np.float32)
    block[:D, :D] = block[D:, D:] = 1.0 / E
    i_of = _np.arange(P) % PR
    j_of = 4 * _np.arange(NG)[None, :] + _np.arange(P)[:, None] // PR
    gsi, bsi = f["L0_rec_gsi"], f["L0_rec_bsi"]
    one, zero = _np.ones((), gsi.dtype), _np.zeros((), gsi.dtype)
    mask9 = _np.zeros((P, 6), _np.float32)
    for r in range(9):
        mask9[r, r // 3] = mask9[r, 3 + r % 3] = 1.0
    cols = {
        "ident": _np.eye(P), "block": block,
        "wst": _np.concatenate([f["L0_rec_Ws"].T] * 2, 0),
        "wssel": wsi.T[rn].reshape(P, -1), "selmask": pick.reshape(P, -1),
        "eps": _np.full((P, 1), EPS),
        "gsrep": rep(f["L0_rec_gs"]), "one": _np.ones((P, 1)), "wsirep": rep(wsi), "mask9": mask9,
        "gd": f["L0_rec_gd"][:, None], "bd": f["L0_rec_bd"][:, None],
        "gi": gsi[i_of][:, None], "bi": bsi[i_of][:, None],
        "gj": _np.where(j_of == 0, one, gsi[j_of - 1]), "bj": _np.where(j_of == 0, zero, bsi[j_of - 1]),
        "isi": i_of[:, None] == _np.arange(PR), "isj": (j_of[:, :, None] - 1 == _np.arange(PR)).reshape(P, -1),
        "isx": j_of == 0,
        "b1": f["b_top1"].reshape(-1, P).T, "b2": f["b_top2"].reshape(-1, P).T,
        "gl": f["L0_rec_gl"][:USED].reshape(KD, P).T, "bl": f["L0_rec_bl"][:USED].reshape(KD, P).T,
        "w3": f["W_top3"].reshape(-1, P).T,
    }

    def packed(pack):
        out = _np.zeros((P, sum(n for _, n in pack)), _np.float32)
        at = 0
        for name, n in pack:
            out[:, at:at + n] = cols[name]
            at += n
        return out

    tri = (i_of[:, None] + 1) * i_of[:, None] // 2 + j_of
    wl = _np.where((j_of <= i_of[:, None])[:, :, None], f["L0_rec_Wl"].T[_np.where(j_of <= i_of[:, None], tri, 0)], zero)
    w1 = _np.concatenate([f["W_top1"][:USED], f["W_top1"][MAXD:]], 0)
    arrays = {
        "table": _np.concatenate(tables, 0),
        "lookups": lookups, "starts": starts,
        "bsrep": rep(f["L0_rec_bs"]),
        "pack_a": packed(PACK_A), "pack_b": packed(PACK_B),
        "wdt": f["L0_rec_Wd"].T.reshape(KR, P, E).transpose(1, 0, 2),
        "denset": f["r_dense_t"].T.reshape(KR, P, B).transpose(1, 0, 2),
        "wlt": wl,
        "w1": w1.reshape(KW, P, H1).transpose(1, 0, 2),
        "w2": f["W_top2"].reshape(H1 // P, P, H2).transpose(1, 0, 2),
    }
    arrays = {k: _np.ascontiguousarray(v) for k, v in arrays.items()}
    nc = _bacc.Bacc("TRN2", target_bir_lowering=False, num_devices=1)
    args = {k: nc.dram_tensor(k, v.shape, _mybir.dt.from_np(v.dtype), kind="ExternalInput").ap()
            for k, v in arrays.items()}
    out = nc.dram_tensor("out", (1, B), _mybir.dt.float32, kind="ExternalOutput").ap()
    build(nc, out=out, **args)
    r = _run(nc, [arrays], core_ids=[0])
    return _np.asarray(r.results[0]["out"]).reshape(B, 1)
```
